# Optimizing a Trainium2 kernel written in Bass

```python
import numpy as np
import jax
import jax.numpy as jnp

def _softmax(x, axis=-1):
    return jax.nn.softmax(x, axis=axis)

def _gelu(x):
    return jax.nn.gelu(x, approximate=True)

def _silu(x):
    return jax.nn.silu(x)

def _sigmoid(x):
    return jax.nn.sigmoid(x)

def _layernorm(x, axis=-1, eps=1e-05):
    m = jnp.mean(x, axis=axis, keepdims=True)
    v = jnp.var(x, axis=axis, keepdims=True)
    return (x - m) / jnp.sqrt(v + eps)

def _scatter_add(tgt, idx, src, axis=0):
    return tgt.at[idx].add(src)

def _segment_sum(src, seg, n):
    return jax.ops.segment_sum(src, seg, n)
kernel_name = 'mk_adj_resnorm_d1_adj_r2_d5c88d'

def setup_inputs(seed: int=0):
    np.random.seed(seed)
    _w = jnp.asarray

    def _rec_inputs():
        import jax
        import jax.numpy as jnp
        _gk = jax.random.key(seed)
        x = -0.0005207 + 1.001 * jax.random.normal(jax.random.fold_in(_gk, 1), (2048, 256), jnp.float32)
        _a = jax.random.bernoulli(jax.random.fold_in(_gk, 2), 0.00390625, (2048, 2048))
        _a = jnp.logical_or(_a, jnp.swapaxes(_a, -1, -2))
        _a = jnp.logical_or(_a, jnp.eye(2048, dtype=bool))
        adj = _a.astype(jnp.int32)
        return (x, adj)
    x, adj = _rec_inputs()

    def _L0_gnn_setup():
        import jax, jax.numpy as jnp
        import numpy as np
        N = 2048
        STATE_DIM = 256
        OUTPUT_DIM = 256
        N_STEPS = 5
        W_STD = 0.02

        def _lin_params(key, out_dim, in_dim):
            W = jax.random.normal(key, (out_dim, in_dim), dtype=jnp.float32) * W_STD
            b = jnp.zeros((out_dim,), dtype=jnp.float32)
            return (W, b)
        key = jax.random.key(seed)
        ks = jax.random.split(key, 10)
        prop_state = jax.random.normal(ks[0], (N, STATE_DIM), dtype=jnp.float32)
        A = jax.random.randint(ks[1], (N, N), 0, 2, dtype=jnp.int64)
        in_W, in_b = _lin_params(ks[2], STATE_DIM, STATE_DIM)
        out_W, out_b = _lin_params(ks[3], STATE_DIM, STATE_DIM)
        r_W, r_b = _lin_params(ks[4], STATE_DIM, 3 * STATE_DIM)
        z_W, z_b = _lin_params(ks[5], STATE_DIM, 3 * STATE_DIM)
        h_W, h_b = _lin_params(ks[6], STATE_DIM, 3 * STATE_DIM)
        o1_W, o1_b = _lin_params(ks[7], STATE_DIM, STATE_DIM)
        o2_W, o2_b = _lin_params(ks[8], OUTPUT_DIM, STATE_DIM)
        return {'prop_state': prop_state, 'A': A, 'in_W': in_W, 'in_b': in_b, 'out_W': out_W, 'out_b': out_b, 'r_W': r_W, 'r_b': r_b, 'z_W': z_W, 'z_b': z_b, 'h_W': h_W, 'h_b': h_b, 'o1_W': o1_W, 'o1_b': o1_b, 'o2_W': o2_W, 'o2_b': o2_b}
    _L0_gnn_all = _L0_gnn_setup()
    _L0_gnn_in = {k: v for k, v in _L0_gnn_all.items() if k in ('in_W', 'in_b', 'out_W', 'out_b', 'r_W', 'r_b', 'z_W', 'z_b', 'h_W', 'h_b', 'o1_W', 'o1_b', 'o2_W', 'o2_b')}
    del _L0_gnn_all
    return {'x': x, 'adj': adj, 'L0_gnn_in_W': _L0_gnn_in['in_W'], 'L0_gnn_in_b': _L0_gnn_in['in_b'], 'L0_gnn_out_W': _L0_gnn_in['out_W'], 'L0_gnn_out_b': _L0_gnn_in['out_b'], 'L0_gnn_r_W': _L0_gnn_in['r_W'], 'L0_gnn_r_b': _L0_gnn_in['r_b'], 'L0_gnn_z_W': _L0_gnn_in['z_W'], 'L0_gnn_z_b': _L0_gnn_in['z_b'], 'L0_gnn_h_W': _L0_gnn_in['h_W'], 'L0_gnn_h_b': _L0_gnn_in['h_b'], 'L0_gnn_o1_W': _L0_gnn_in['o1_W'], 'L0_gnn_o1_b': _L0_gnn_in['o1_b'], 'L0_gnn_o2_W': _L0_gnn_in['o2_W'], 'L0_gnn_o2_b': _L0_gnn_in['o2_b']}

def reference(x, adj, L0_gnn_in_W, L0_gnn_in_b, L0_gnn_out_W, L0_gnn_out_b, L0_gnn_r_W, L0_gnn_r_b, L0_gnn_z_W, L0_gnn_z_b, L0_gnn_h_W, L0_gnn_h_b, L0_gnn_o1_W, L0_gnn_o1_b, L0_gnn_o2_W, L0_gnn_o2_b):
    import jax
    import jax.numpy as jnp

    def _L0_gnn_ref(prop_state, A, in_W, in_b, out_W, out_b, r_W, r_b, z_W, z_b, h_W, h_b, o1_W, o1_b, o2_W, o2_b):
        import jax, jax.numpy as jnp
        import numpy as np
        N = 2048
        STATE_DIM = 256
        OUTPUT_DIM = 256
        N_STEPS = 5
        W_STD = 0.02

        def _lin_params(key, out_dim, in_dim):
            W = jax.random.normal(key, (out_dim, in_dim), dtype=jnp.float32) * W_STD
            b = jnp.zeros((out_dim,), dtype=jnp.float32)
            return (W, b)
        Af = A.astype(prop_state.dtype)
        AfT = Af.T
        state = prop_state
        for _ in range(N_STEPS):
            s_in = state @ in_W.T + in_b
            s_out = state @ out_W.T + out_b
            a_in = Af @ s_in
            a_out = AfT @ s_out
            a = jnp.concatenate([a_in, a_out, state], axis=-1)
            r = jax.nn.sigmoid(a @ r_W.T + r_b)
            z = jax.nn.sigmoid(a @ z_W.T + z_b)
            joined = jnp.concatenate([a_in, a_out, r * state], axis=-1)
            h_hat = jnp.tanh(joined @ h_W.T + h_b)
            state = (1.0 - z) * state + z * h_hat
        out = jnp.tanh(state @ o1_W.T + o1_b) @ o2_W.T + o2_b
        return out
    x = _layernorm(x + _L0_gnn_ref(x, adj, L0_gnn_in_W, L0_gnn_in_b, L0_gnn_out_W, L0_gnn_out_b, L0_gnn_r_W, L0_gnn_r_b, L0_gnn_z_W, L0_gnn_z_b, L0_gnn_h_W, L0_gnn_h_b, L0_gnn_o1_W, L0_gnn_o1_b, L0_gnn_o2_W, L0_gnn_o2_b), axis=-1)
    return x

_drawn_inputs = setup_inputs


def setup_inputs(seed=0):
    import zlib

    import numpy as np

    out = dict(_drawn_inputs(seed))
    spreads = {'L0_gnn_in_b': (0.0, 0.298),
     'L0_gnn_out_b': (0.0, 0.1),
     'L0_gnn_r_b': (0.0, 2.0),
     'L0_gnn_z_b': (0.0, 2.0),
     'L0_gnn_h_b': (0.0, 0.8),
     'L0_gnn_o1_b': (0.0, 0.1),
     'L0_gnn_o2_b': (0.0, 0.1)}
    factors = {'L0_gnn_r_W': 200.0}
    for name, (base, spread) in spreads.items():
        noise = np.random.default_rng([zlib.crc32(name.encode()), seed]).standard_normal(out[name].shape)
        drawn = base * np.exp(spread * noise) if base else spread * noise
        out[name] = jnp.asarray(drawn.astype(out[name].dtype))
    for name, factor in factors.items():
        out[name] = (out[name] * factor).astype(out[name].dtype)
    return out
```

```python
from contextlib import ExitStack

import concourse.bass as bass
from concourse import mybir

F32 = mybir.dt.float32
I32 = mybir.dt.int32
ALU = mybir.AluOpType
ACT = mybir.ActivationFunctionType

P = 128
CW = 512
EPS = 1e-5
N_STEPS = 5


def gnn_kernel(nc, x, adj, in_W, in_b, out_W, out_b, r_W, r_b, z_W, z_b, h_W, h_b,
               o1_W, o1_b, o2_W, o2_b, out):
    N, D = x.shape
    NB = N // P
    NC = N // CW
    DB = D // P
    BC = CW // P
    NG = 3
    KB = NG * DB
    R, Z, H = range(NG)

    with ExitStack() as ctx:
        def sb(name, shape, dt=F32):
            return ctx.enter_context(nc.sbuf_tensor(name, shape, dt))

        def pb(name, shape, dt=F32):
            return ctx.enter_context(nc.psum_tensor(name, shape, dt))

        def sem(name):
            return ctx.enter_context(nc.semaphore(name))

        a_dram = nc.dram_tensor("a_dram", [N, N], F32, kind="Internal").ap()
        at_dram = nc.dram_tensor("at_dram", [N, N], F32, kind="Internal").ap()

        ident = sb("ident", [P, P])
        xb = sb("xb", [P, NB, D])
        stateT = sb("stateT", [P, DB, N])
        lin_raw = sb("lin_raw", [P, 4, DB, D])
        lin_T = sb("lin_T", [P, 4, DB, D])
        gate_raw = sb("gate_raw", [P, DB, NG * D])
        gate_T = sb("gate_T", [P, NG, KB, D])
        gate_b = sb("gate_b", [P, NG, DB])
        o1_bc = sb("o1_bc", [P, DB])
        io_b = sb("io_b", [P, 2 * D])
        o2_bb = sb("o2_bb", [P, D])
        s_io = sb("s_io", [P, NB, 2 * D])
        a_io = sb("a_io", [P, 4, CW])
        gates = sb("gates", [P, NG, DB, CW])
        rs = sb("rs", [P, DB, CW])
        tmp = sb("tmp", [P, DB, CW])
        tile = sb("tile", [P, 2, 2, 2, CW])
        y = sb("y", [P, BC, D])
        stats = sb("stats", [P, BC, 6])
        mv = sb("mv", [P, BC, 2])
        rstd = sb("rstd", [P, BC])
        araw = s_io[:, 0:4, :].bitcast(I32)
        af = s_io[:, 4:8, :]
        att = s_io[:, 8:12, :]

        bank = [pb(f"bank{i}", [P, CW]) for i in range(8)]

        loaded = sem("loaded")
        ident_zeroed = sem("ident_zeroed")
        ident_ready = sem("ident_ready")
        prep_done = sem("prep_done")
        prep_copied = sem("prep_copied")
        gate_loaded = sem("gate_loaded")
        gate_used = sem("gate_used")
        xb_ready = sem("xb_ready")
        araw_loaded = sem("araw_loaded")
        af_ready = sem("af_ready")
        at_done = sem("at_done")
        att_ready = sem("att_ready")
        a_stored = sem("a_stored")
        proj_done = sem("proj_done")
        proj_read = sem("proj_read")
        tile_loaded = [sem(f"tile_loaded{i}") for i in range(2)]
        tile_used = sem("tile_used")
        agg_done = sem("agg_done")
        agg_read = sem("agg_read")
        gate_done = sem("gate_done")
        gate_read = sem("gate_read")
        rs_ready = sem("rs_ready")
        link = sem("link")
        state_ready = sem("state_ready")
        hid_done = sem("hid_done")
        hid_ready = sem("hid_ready")
        o_done = sem("o_done")
        o_read = sem("o_read")
        var_ready = sem("var_ready")
        std_ready = sem("std_ready")
        y_ready = sem("y_ready")
        y_stored = sem("y_stored")

        block = ctx.enter_context(nc.Block())

        LOADS = 4 + 3 * 1 + 1 + 2 + 1 + 1
        NLIN = 4 * DB
        x_v = x.rearrange("(b p) d -> p b d", p=P)

        @block.sync
        def _(sp):
            for n, w in enumerate((in_W, out_W, o1_W, o2_W)):
                sp.dma_start(lin_raw[:, n], w.rearrange("(b p) k -> p b k", p=P)).then_inc(loaded, 16)
            for g, b in enumerate((r_b, z_b, h_b)):
                sp.dma_start(gate_b[:, g], b.rearrange("(b p) -> p b", p=P), allow_slow_non_contiguous=True).then_inc(loaded, 16)
            sp.dma_start(o1_bc[:, :], o1_b.rearrange("(b p) -> p b", p=P), allow_slow_non_contiguous=True).then_inc(loaded, 16)
            sp.dma_start(io_b[:, 0:D], in_b.partition_broadcast(P)).then_inc(loaded, 16)
            sp.dma_start(io_b[:, D:], out_b.partition_broadcast(P)).then_inc(loaded, 16)
            sp.dma_start(o2_bb[:, :], o2_b.partition_broadcast(P)).then_inc(loaded, 16)
            sp.dma_start(xb[:, :, :], x_v).then_inc(loaded, 16)
            for g, w in enumerate((r_W, z_W, h_W)):
                if g:
                    sp.wait_ge(gate_used, g)
                sp.dma_start(gate_raw[:, :, :], w.rearrange("(b p) k -> p b k", p=P)).then_inc(gate_loaded, 16)
            with sp.Fori(0, NB) as b:
                column = sp.snap(b * P)
                sp.wait_ge(a_stored, 1 + b * 32)
                sp.dma_start(araw, adj[bass.ds(b * P, P), :].rearrange("p (c w) -> p c w", c=NC)).then_inc(araw_loaded, 16)
                sp.wait_ge(att_ready, 1 + (b + 1) * NC)
                sp.dma_start(a_dram[bass.ds(b * P, P), :].rearrange("p (c w) -> p c w", c=NC), af).then_inc(a_stored, 16)
                sp.dma_start(at_dram[:, bass.ds(column, P)].rearrange("(j p) i -> p j i", p=P),
                             att.rearrange("p c (j i) -> p (c j) i", i=P)).then_inc(a_stored, 16)
            sp.wait_ge(a_stored, 1 + NB * 32)
            a_v = a_dram.rearrange("(j p) i -> p j i", p=P)
            at_v = at_dram.rearrange("(j p) i -> p j i", p=P)
            with sp.Fori(0, N_STEPS * NC) as q:
                col = sp.snap((q % NC) * CW)
                for j in range(NB // 2):
                    n = q * (NB // 2) + j
                    if j >= 2:
                        sp.wait_ge(tile_used, 1 + n - 1)
                    else:
                        sp.wait_ge(tile_used, 1 + q * (NB // 2))
                    for m, v in enumerate((at_v, a_v)):
                        sp.dma_start(tile[:, j % 2, m], v[:, 2 * j:2 * j + 2, bass.ds(col, CW)])\
                          .then_inc(tile_loaded[j % 2], 16)
            with sp.Fori(0, NC) as c:
                sp.wait_ge(y_ready, (c + 1) * BC)
                sp.dma_start(out.rearrange("(b p) d -> p b d", p=P)[:, bass.ds(c * BC, BC), :], y[:, :, :]).then_inc(y_stored, 16)
            sp.wait_ge(y_stored, 16 * NC)

        @block.gpsimd
        def _(pool):
            for s in (a_stored, tile_used, att_ready, state_ready, agg_read, gate_read, hid_ready, o_read, o_done):
                pool.sem_inc(s, 1)
            nc.gpsimd.memset(ident[:, :], 0.0).then_inc(ident_zeroed, 1)
            pool.wait_ge(ident_zeroed, 1)
            nc.gpsimd.affine_select(out=ident[:, :], in_=ident[:, :], compare_op=ALU.not_equal, fill=1.0,
                                    base=0, pattern=[[-1, P]], channel_multiplier=1).then_inc(ident_ready, 1)

        @block.tensor
        def _(pe):
            pe.wait_ge(ident_ready, 1)
            pe.wait_ge(loaded, 16 * LOADS)
            n = 0
            for w in range(4):
                for k in range(DB):
                    if n >= 8:
                        pe.wait_ge(prep_copied, n - 7)
                    for b in range(DB):
                        last = nc.tensor.transpose(bank[n % 8][:, b * P:(b + 1) * P], lin_raw[:, w, b, k * P:(k + 1) * P], ident[:, :])
                    last.then_inc(prep_done, 1)
                    n += 1
            for g in range(NG):
                pe.wait_ge(gate_loaded, 16 * (g + 1))
                for k in range(KB):
                    if n >= 8:
                        pe.wait_ge(prep_copied, n - 7)
                    for b in range(DB):
                        last = nc.tensor.transpose(bank[n % 8][:, b * P:(b + 1) * P], gate_raw[:, b, k * P:(k + 1) * P], ident[:, :])
                    last.then_inc(prep_done, 1)
                    n += 1
            for d in range(DB):
                for c in range(NC):
                    pe.wait_ge(prep_copied, n - 7)
                    for b in range(BC):
                        last = nc.tensor.transpose(bank[n % 8][:, b * P:(b + 1) * P], xb[:, c * BC + b, d * P:(d + 1) * P], ident[:, :])
                    last.then_inc(prep_done, 1)
                    n += 1
            pe.wait_ge(prep_copied, n)
            with pe.Fori(0, NB) as b:
                pe.wait_ge(af_ready, b + 1)
                pe.wait_ge(att_ready, 1 + b * NC)
                for c in range(NC):
                    for j in range(BC):
                        last = nc.tensor.transpose(bank[c][:, j * P:(j + 1) * P], af[:, c, j * P:(j + 1) * P], ident[:, :])
                    last.then_inc(at_done, 1)
            pe.wait_ge(att_ready, 1 + NB * NC)
            pe.wait_ge(a_stored, 1 + NB * 32)
            with pe.Fori(0, N_STEPS) as t:
                pe.wait_ge(state_ready, 1 + t * NC * DB)
                for b in range(NB):
                    if b >= 2:
                        pe.wait_ge(proj_read, t * NB + b - 1)
                    for k in range(DB):
                        last = nc.tensor.matmul(bank[b % 2][:, :], stateT[:, k, b * P:(b + 1) * P],
                                                lin_T[:, 0:2, k, :], start=(k == 0), stop=(k == DB - 1))
                    last.then_inc(proj_done, 1)
                with pe.Fori(0, NC) as c:
                    q = t * NC + c
                    pe.wait_ge(proj_read, (t + 1) * NB)
                    pe.wait_ge(agg_read, 1 + 4 * q)
                    for j in range(NB):
                        if j % 2 == 0:
                            pe.wait_ge(tile_loaded[j // 2 % 2], 32 * (q * (NB // 4) + j // 4 + 1))
                        for m in range(2):
                            for d in range(DB):
                                last = nc.tensor.matmul(bank[2 + m * DB + d][:, :],
                                                        s_io[:, j, m * D + d * P:m * D + (d + 1) * P],
                                                        tile[:, j // 2 % 2, m, j % 2, :],
                                                        start=(j == 0), stop=(j == NB - 1))
                        if j == NB - 1:
                            last.then_inc(agg_done, 1)
                        if j % 2 == 1:
                            if j == NB - 1:
                                pe.wait_ge(agg_done, q + 1)
                                pe.sem_inc(tile_used, 1)
                            else:
                                last.then_inc(tile_used, 1)
                    pe.wait_ge(agg_read, 1 + 4 * (q + 1))
                    for s in range(NG * DB):
                        g, e = s // DB, s % DB
                        pe.wait_ge(gate_read, 1 + q * NG * DB + (s - 1 if s >= 2 else 0))
                        for k in range(KB):
                            if k < 4:
                                rhs = a_io[:, k, :]
                            elif g == H:
                                if k == 4:
                                    pe.wait_ge(rs_ready, (q + 1) * DB)
                                rhs = rs[:, k - 4, :]
                            else:
                                rhs = stateT[:, k - 4, bass.ds(c * CW, CW)]
                            last = nc.tensor.matmul(bank[6 + s % 2][:, :], gate_T[:, g, k, e * P:(e + 1) * P], rhs,
                                                    start=(k == 0), stop=(k == KB - 1))
                        last.then_inc(gate_done, 1)
            pe.wait_ge(state_ready, 1 + N_STEPS * NC * DB)
            pe.wait_ge(gate_read, 1 + N_STEPS * NC * NG * DB)
            with pe.Fori(0, NC) as c:
                pe.wait_ge(hid_ready, 1 + c * DB)
                for e in range(DB):
                    for k in range(DB):
                        last = nc.tensor.matmul(bank[e][:, :], lin_T[:, 2, k, e * P:(e + 1) * P],
                                                stateT[:, k, bass.ds(c * CW, CW)], start=(k == 0), stop=(k == DB - 1))
                    last.then_inc(hid_done, 1)
                pe.wait_ge(hid_ready, 1 + (c + 1) * DB)
                pe.wait_ge(o_read, 1 + c * BC)
                for b in range(BC):
                    for k in range(DB):
                        last = nc.tensor.matmul(bank[2 + b][:, 0:D], rs[:, k, b * P:(b + 1) * P],
                                                lin_T[:, 3, k, :], start=(k == 0), stop=(k == DB - 1))
                    last.then_inc(o_done, 1)

        @block.scalar
        def _(act):
            with act.Fori(0, N_STEPS * NC) as q:
                act.wait_ge(state_ready, 1 + q * DB)
                for s in range(NG * DB):
                    g, e = s // DB, s % DB
                    act.wait_ge(gate_done, q * NG * DB + s + 1)
                    nc.scalar.activation(gates[:, g, e, :], bank[6 + s % 2][:, :], ACT.Tanh if g == H else ACT.Sigmoid,
                                         bias=gate_b[:, g, e:e + 1]).then_inc(gate_read, 1)
            with act.Fori(0, NC) as c:
                act.wait_ge(o_done, 1 + c * BC)
                for e in range(DB):
                    act.wait_ge(hid_done, c * DB + e + 1)
                    nc.scalar.activation(rs[:, e, :], bank[e][:, :], ACT.Tanh, bias=o1_bc[:, e:e + 1]).then_inc(hid_ready, 1)
                act.wait_ge(var_ready, c + 1)
                nc.scalar.activation(rstd[:, :], mv[:, :, 1], ACT.Sqrt).then_inc(std_ready, 1)

        @block.vector
        def _(dve):
            n = 0
            for w in range(4):
                for k in range(DB):
                    dve.wait_ge(prep_done, n + 1)
                    nc.vector.tensor_copy(lin_T[:, w, k, :], bank[n % 8][:, 0:D]).then_inc(prep_copied, 1)
                    n += 1
            for g in range(NG):
                for k in range(KB):
                    dve.wait_ge(prep_done, n + 1)
                    if k == KB - 1:
                        dve.sem_inc(gate_used, 1)
                    nc.vector.tensor_copy(gate_T[:, g, k, :], bank[n % 8][:, 0:D]).then_inc(prep_copied, 1)
                    n += 1
            for d in range(DB):
                for c in range(NC):
                    dve.wait_ge(prep_done, n + 1)
                    nc.vector.tensor_copy(stateT[:, d, c * CW:(c + 1) * CW], bank[n % 8][:, :]).then_inc(prep_copied, 1)
                    n += 1
            nc.vector.tensor_tensor(xb[:, :, :], xb[:, :, :], o2_bb[:, :].unsqueeze(1).broadcast_to([P, NB, D]), ALU.add).then_inc(xb_ready, 1)
            with dve.Fori(0, NB) as b:
                dve.wait_ge(araw_loaded, 16 * (b + 1))
                nc.vector.tensor_copy(af, araw).then_inc(af_ready, 1)
                for c in range(NC):
                    dve.wait_ge(at_done, b * NC + c + 1)
                    nc.vector.tensor_copy(att[:, c, :], bank[c][:, :]).then_inc(att_ready, 1)
            dve.wait_ge(a_stored, 1 + NB * 32)
            with dve.Fori(0, N_STEPS) as t:
                for b in range(NB):
                    dve.wait_ge(proj_done, t * NB + b + 1)
                    nc.vector.tensor_tensor(s_io[:, b, :], bank[b % 2][:, :], io_b[:, :], ALU.add).then_inc(proj_read, 1)
                with dve.Fori(0, NC) as c:
                    q = t * NC + c
                    dve.wait_ge(agg_done, q + 1)
                    for k in range(4):
                        nc.vector.tensor_copy(a_io[:, k, :], bank[2 + k][:, :]).then_inc(agg_read, 1)
                    st = stateT[:, :, bass.ds(c * CW, CW)]
                    for e in range(DB):
                        dve.wait_ge(gate_read, 1 + q * NG * DB + e + 1)
                        nc.vector.tensor_tensor(rs[:, e, :], gates[:, R, e, :], stateT[:, e, bass.ds(c * CW, CW)], ALU.mult).then_inc(rs_ready, 1)
                    for e in range(DB):
                        se = stateT[:, e, bass.ds(c * CW, CW)]
                        u = 2 * (q * DB + e)
                        dve.wait_ge(gate_read, 1 + q * NG * DB + H * DB + e + 1)
                        nc.vector.tensor_tensor(tmp[:, e, :], gates[:, H, e, :], se, ALU.subtract).then_inc(link, 1)
                        dve.wait_ge(link, u + 1)
                        nc.vector.tensor_tensor(tmp[:, e, :], tmp[:, e, :], gates[:, Z, e, :], ALU.mult).then_inc(link, 1)
                        dve.wait_ge(link, u + 2)
                        nc.vector.tensor_tensor(se, se, tmp[:, e, :], ALU.add).then_inc(state_ready, 1)
            link0 = 2 * N_STEPS * NC * DB
            LN = 2 * BC + 1 + 2
            for c in range(NC):
                if c:
                    dve.wait_ge(y_stored, 16 * c)
                at = link0 + c * LN
                for b in range(BC):
                    dve.wait_ge(o_done, 1 + c * BC + b + 1)
                    nc.vector.tensor_tensor(y[:, b, :], bank[2 + b][:, 0:D], xb[:, c * BC + b, :], ALU.add).then_inc(o_read, 1)
                for b in range(BC):
                    dve.wait_ge(o_read, 1 + c * BC + b + 1)
                    nc.vector.bn_stats(stats[:, b, :], y[:, b, :]).then_inc(link, 1)
                for b in range(BC):
                    dve.wait_ge(link, at + b + 1)
                    nc.vector.bn_aggr(mv[:, b, :], stats[:, b, :]).then_inc(link, 1)
                dve.wait_ge(link, at + 2 * BC)
                nc.vector.tensor_scalar(mv[:, :, 1], mv[:, :, 1], EPS, None, ALU.add).then_inc(var_ready, 1)
                dve.wait_ge(std_ready, c + 1)
                nc.vector.reciprocal(rstd[:, :], rstd[:, :]).then_inc(link, 3)
                dve.wait_ge(link, at + 2 * BC + 3)
                for b in range(BC):
                    nc.vector.tensor_scalar(y[:, b, :], y[:, b, :], mv[:, b, 0:1], rstd[:, b:b + 1], ALU.subtract, ALU.mult).then_inc(y_ready, 1)


_INS = ["x", "adj"] + ["L0_gnn_" + n for n in ("in_W", "in_b", "out_W", "out_b", "r_W", "r_b", "z_W", "z_b", "h_W", "h_b",
                                              "o1_W", "o1_b", "o2_W", "o2_b")]


def kernel(**inputs):
    import numpy as _np
    import concourse.bacc as _bacc
    from concourse import mybir as _mybir
    from concourse.bass_utils import run_bass_kernel_spmd as _run

    nc = _bacc.Bacc("TRN2", target_bir_lowering=False, num_devices=1)
    arrays, args = {}, []
    for name in _INS:
        a = _np.ascontiguousarray(inputs[name])
        arrays[f"in_{name}_dram"] = a
        args.append(nc.dram_tensor(f"in_{name}_dram", a.shape, _mybir.dt.from_np(a.dtype), kind="ExternalInput").ap())
    out = nc.dram_tensor("out_0_dram", inputs["x"].shape, _mybir.dt.float32, kind="ExternalOutput").ap()
    gnn_kernel(nc, *args, out)
    r = _run(nc, [arrays], core_ids=[0])
    return r.results[0]["out_0_dram"]
```

```python
from contextlib import ExitStack

import concourse.bass as bass
from concourse import mybir

F32 = mybir.dt.float32
F32R = mybir.dt.float32r
I32 = mybir.dt.int32
U32 = mybir.dt.uint32
U16 = mybir.dt.uint16
U8 = mybir.dt.uint8
ALU = mybir.AluOpType
ACT = mybir.ActivationFunctionType

P = 128
CW = 512
EPS = 1e-5
N_STEPS = 5
MISMATCHES = 1 << 23


def wait(eng, sem, value):
    if not isinstance(value, int) or value > 0:
        eng.wait_ge(sem, value)


def fast_path(nc, flag, x, adj, in_W, in_b, out_W, out_b, r_W, r_b, z_W, z_b, h_W, h_b,
              o1_W, o1_b, o2_W, o2_b, out):
    N, D = x.shape
    NB, NC, DB = N // P, N // CW, D // P
    BC = CW // P
    NG, NK = 3, 3 * DB
    R, Z, H = range(NG)
    HI, LO = range(2)
    NP = NB // 2
    RING, STAGES = 4, 3
    LEAD = RING
    LAST = N_STEPS - 1

    S_GATE = NC * NG * DB
    GATE = NG * DB
    S_TWO, TWO = NC * DB, DB
    S_PAIR = NC * NP

    T_AT = {(2, 0): (0, 0), (2, 1): (0, 1), (2, 2): (1, 0), (2, 3): (1, 1), (3, 2): (2, 0), (3, 3): (2, 1)}

    with ExitStack() as ctx:
        def sb(name, shape, dt=F32):
            return ctx.enter_context(nc.sbuf_tensor(name, shape, dt))

        def sem(name):
            return ctx.enter_context(nc.semaphore(name))

        ident = sb("ident", [P, P])
        ones = sb("ones", [P, P])
        ones_r = sb("ones_r", [P, P], F32R)
        rows = sb("rows", [P, 2, NB, D], F32R)
        stateT = sb("stateT", [P, DB, N])
        fold = sb("fold", [P, 2, DB, NG, D], F32R)
        own = sb("own", [P, 2, DB, NG, D], F32R)
        o_w = sb("o_w", [P, 2, 2, DB, D], F32R)
        a8 = sb("a8", [P, NC, NB, CW], U8)
        ring = sb("ring", [P, RING, 2, CW], F32R)
        stage = sb("stage", [P, STAGES, 2, CW], I32)
        degree = sb("degree", [P, N], U16)
        st_c = sb("st_c", [P, 2, DB, CW], F32R)
        u_c = sb("u_c", [P, 2, DB, CW], F32R)
        rs_c = sb("rs_c", [P, 2, DB, CW], F32R)
        work = sb("work", [P, 8, CW])
        gates = work[:, 0:6, :].rearrange("p (g e) w -> p g e w", g=NG)
        tmp = work[:, 6:8, :]
        x_raw = work[:, :, :].rearrange("p a w -> p (a w)").rearrange("p (b d) -> p b d", d=D)
        bias = sb("bias", [P, NG + 3, DB])
        deg_w = sb("deg_w", [P, NG, DB])
        o2_bb = sb("o2_bb", [P, D])
        differs = sb("differs", [P, 2, 2 * P], U8)
        stats = sb("stats", [P, NB, 6])
        mv = sb("mv", [P, NB, 2])
        std = sb("std", [P, NB])
        rstd = sb("rstd", [P, NB])
        shift = sb("shift", [P, NB])
        above = sb("above", [P, NC * NP])
        differ = sb("differ", [P, 36])
        odd = sb("odd", [P, 3])

        late = a8[:, 2:4, :, :].rearrange("p c b w -> p (c b w)").bitcast(F32)
        NR = DB * NG * D
        gate_raw = [late[:, 0:NR], late[:, NR:2 * NR], work[:, 0:3, :].rearrange("p a w -> p (a w)")]
        gate_raw = [g.rearrange("p (b k) -> p b k", b=DB) for g in gate_raw]
        o_raw = late[:, 2 * NR:2 * NR + 2 * DB * D].rearrange("p (n b k) -> p n b k", n=2, b=DB)
        gate_T = work[:, 3:5, :].rearrange("p a (m d) -> p (a m) d", d=D)
        lin_raw = work[:, 5:7, :].rearrange("p n (b k) -> p n b k", b=DB)

        y = a8[:, 0:2, :, :].rearrange("p c b w -> p (c b w)").bitcast(F32).rearrange("p (b d) -> p b d", d=D)
        x_res = late.rearrange("p (b d) -> p b d", d=D)
        hid = gates[:, R, :, :]
        hid_c = [[rs_c[:, HI], rs_c[:, LO]], [ring[:, HI], ring[:, LO]]]

        bank = [ctx.enter_context(nc.psum_tensor(f"bank{i}", [P, CW], F32)) for i in range(8)]
        u_bank = bank[0:4]
        g_bank = bank[4:7]
        t_bank = bank[7]
        check_bank = [t_bank, g_bank[1]]
        out_bank = [bank[2], bank[3], bank[4], bank[5]]

        stage_loaded = [sem(f"f_stage_loaded{i}") for i in range(STAGES)]
        x_loaded = sem("f_x_loaded")
        small_loaded = sem("f_small_loaded")
        w_loaded = sem("f_w_loaded")
        zeroed = sem("f_zeroed")
        const_ready = sem("f_const_ready")
        ones_ready = sem("f_ones_ready")
        x_hi = sem("f_x_hi")
        x_split = sem("f_x_split")
        x_turned = sem("f_x_turned")
        state0 = sem("f_state0")
        prep_done = sem("f_prep_done")
        prep_hi = sem("f_prep_hi")
        prep_read = sem("f_prep_read")
        pair_stored = sem("f_pair_stored")
        pair_ready = sem("f_pair_ready")
        pair_used = sem("f_pair_used")
        check_done = sem("f_check_done")
        check_read = sem("f_check_read")
        degree_read = sem("f_degree_read")
        agg_done = sem("f_agg_done")
        u_hi = sem("f_u_hi")
        u_lo = sem("f_u_lo")
        u_used = sem("f_u_used")
        st_hi = sem("f_st_hi")
        st_lo = sem("f_st_lo")
        gate_done = sem("f_gate_done")
        gate_read = sem("f_gate_read")
        gate_act = sem("f_gate_act")
        rs_ready = sem("f_rs_ready")
        rs_hi = sem("f_rs_hi")
        rs_lo = sem("f_rs_lo")
        turn_done = sem("f_turn_done")
        row_hi = sem("f_row_hi")
        row_lo = sem("f_row_lo")
        state_new = sem("f_state_new")
        chain = sem("f_chain")
        fin_link = sem("f_fin_link")
        odd_ready = sem("f_odd_ready")
        odd_done = sem("f_odd_done")
        hid_done = sem("f_hid_done")
        hid_act = sem("f_hid_act")
        hid_hi = sem("f_hid_hi")
        hid_lo = sem("f_hid_lo")
        o_done = sem("f_o_done")
        o_read = sem("f_o_read")
        xr_loaded = sem("f_xr_loaded")
        residual_ready = sem("f_residual_ready")
        stats_ready = sem("f_stats_ready")
        aggr_ready = sem("f_aggr_ready")
        std_first = sem("f_std_first")
        shift_ready = sem("f_shift_ready")
        y_last = sem("f_y_last")
        var_ready = sem("f_var_ready")
        std_ready = sem("f_std_ready")
        y_ready = sem("f_y_ready")
        y_stored = sem("f_y_stored")

        NPREP_G = 3
        out_v = out.rearrange("(b p) d -> p b d", p=P)
        x_v = x.rearrange("(b p) d -> p b d", p=P)
        adj_v = adj.rearrange("(j p) i -> p j i", p=P)
        N_SMALL = NG + 3 + 1
        checks = [(c, p, h) for c in range(NC) for p in range(2 * c + 2) for h in range(1 if p == 2 * c else 2)]

        block = ctx.enter_context(nc.Block())

        @block.sync
        def _(sp):
            sp.dma_start(x_raw, x_v).then_inc(x_loaded, 16)
            for c in range(NC):
                for p in range(NP):
                    q = c * NP + p
                    if q >= STAGES:
                        sp.wait_ge(pair_ready, q - STAGES + 1)
                        sp.wait_ge(pair_stored, q - STAGES + 1)
                    sp.dma_start(stage[:, q % STAGES], adj_v[:, 2 * p:2 * p + 2, c * CW:(c + 1) * CW])\
                      .then_inc(stage_loaded[q % STAGES], 16)
            sp.wait_ge(pair_ready, N_STEPS * S_PAIR)
            sp.dma_start(x_res, x_v).then_inc(xr_loaded, 16)
            for c in range(NC):
                sp.wait_ge(y_ready, c + 1)
                sp.wait_ge(y_last, c + 1)
                sp.dma_start(out_v[:, c * BC:(c + 1) * BC, :], y[:, c * BC:(c + 1) * BC, :]).then_inc(y_stored, 16)
            sp.wait_ge(y_stored, 16 * NC)

        @block.gpsimd
        def _(pool):
            nc.gpsimd.memset(ident[:, :], 0.0).then_inc(zeroed, 1)
            nc.gpsimd.memset(ones[:, :], 1.0).then_inc(const_ready, 1)
            pool.wait_ge(zeroed, 1)
            nc.gpsimd.affine_select(out=ident[:, :], in_=ident[:, :], compare_op=ALU.not_equal, fill=1.0,
                                    base=0, pattern=[[-1, P]], channel_multiplier=1).then_inc(const_ready, 1)
            for n, b in enumerate((r_b, z_b, h_b, o1_b, in_b, out_b)):
                pool.dma_start(bias[:, n], b.rearrange("(b p) -> p b", p=P), allow_slow_non_contiguous=True)\
                    .then_inc(small_loaded, 16)
            pool.dma_start(o2_bb[:, :], o2_b.partition_broadcast(P)).then_inc(small_loaded, 16)
            pool.wait_ge(x_loaded, 16)
            for g, w in ((R, r_W), (Z, z_W)):
                pool.dma_start(gate_raw[g], w.rearrange("(b p) k -> p b k", p=P)).then_inc(w_loaded, 16)
            for n, w in enumerate((o1_W, o2_W)):
                pool.dma_start(o_raw[:, n], w.rearrange("(b p) k -> p b k", p=P)).then_inc(w_loaded, 16)
            pool.wait_ge(x_turned, DB * NC)
            pool.wait_ge(x_split, NC)
            pool.dma_start(gate_raw[H], h_W.rearrange("(b p) k -> p b k", p=P)).then_inc(w_loaded, 16)
            for n, w in enumerate((in_W, out_W)):
                pool.dma_start(lin_raw[:, n], w.rearrange("(b p) k -> p b k", p=P)).then_inc(w_loaded, 16)
            pool.wait_ge(xr_loaded, 16)
            for c in range(NC):
                xr = x_res[:, c * BC:(c + 1) * BC, :]
                nc.gpsimd.tensor_tensor(xr, xr, o2_bb[:, :].unsqueeze(1).broadcast_to([P, BC, D]), ALU.add)\
                    .then_inc(residual_ready, 1)

        @block.tensor
        def _(pe):
            def three(out_, wh, wl, vh, vl, first, last):
                nc.tensor.matmul(out_, wh, vh, start=first, stop=False)
                nc.tensor.matmul(out_, wh, vl, start=False, stop=False)
                return nc.tensor.matmul(out_, wl, vh, start=False, stop=last)

            def check_block(c, p, h):
                n = checks.index((c, p, h))
                wait(pe, check_read, n - 1)
                for b in range(2):
                    for j in range(2):
                        last = nc.tensor.transpose(
                            check_bank[n % 2][:, (2 * b + j) * P:(2 * b + j + 1) * P],
                            ring[:, p % RING, j, (2 * h + b) * P:(2 * h + b + 1) * P].bitcast(F32), ident[:, :])
                last.then_inc(check_done, 1)

            def turn(t, k, h):
                wait(pe, state_new, t * S_TWO + (k + 1) * TWO)
                wait(pe, row_lo, t * S_TWO + 2 * k + h)
                for j in range(2):
                    for d in range(DB):
                        b = k * BC + 2 * h + j
                        last = nc.tensor.transpose(t_bank[:, (j * DB + d) * P:(j * DB + d + 1) * P],
                                                   stateT[:, d, b * P:(b + 1) * P], ident[:, :])
                last.then_inc(turn_done, 1)

            def aggregate(t, c, first=False):
                wait(pe, u_lo, t * S_TWO + (c - 1) * TWO)
                if first:
                    wait(pe, gate_read, (c - 1) * GATE)
                for p in range(NP):
                    pe.wait_ge(pair_ready, t * S_PAIR + c * NP + p + 1)
                    if c == 0 and not first:
                        if p == 4:
                            turn(t - 1, NC - 1, 0)
                        if p == 5:
                            turn(t - 1, NC - 1, 1)
                        pe.wait_ge(row_lo, (t - 1) * S_TWO + p + 1)
                    if c == 0 and first:
                        pe.wait_ge(x_split, p // 2 + 1)
                    for jj in range(2):
                        j = 2 * p + jj
                        if first and (c, p, jj) in checks:
                            check_block(c, p, jj)
                        if first:
                            nc.tensor.matmul(g_bank[0][:, :], ones_r[:, :], ring[:, p % RING, jj, :],
                                             start=(j == 0), stop=(j == NB - 1))
                        for d in range(DB):
                            for part in (HI, LO):
                                last = nc.tensor.matmul(u_bank[2 * (c % 2) + d][:, :], rows[:, part, j, d * P:(d + 1) * P],
                                                        ring[:, p % RING, jj, :], start=(j == 0 and part == HI),
                                                        stop=(j == NB - 1 and part == LO))
                            if j == NB - 1 and d == 0:
                                last.then_inc(agg_done, 1)
                    last.then_inc(pair_used, 1)
                if first:
                    pe.wait_ge(degree_read, c + 1)
                    pe.wait_ge(check_read, sum(k <= c for k, _, _ in checks))

            def gate_chunk(t, c):
                pe.wait_ge(st_lo, t * S_TWO + (c + 1) * TWO)
                for s in range(2 * DB):
                    g, e = s // DB, s % DB
                    wait(pe, gate_read, t * S_GATE + c * GATE + s - 2)
                    own_part(g_bank[s % 3], g, e, st_c)
                    if s == 0:
                        pe.wait_ge(u_lo, t * S_TWO + (c + 1) * TWO)
                    fold_part(g_bank[s % 3], g, e, False).then_inc(gate_done, 1)
                    if (c, s) in T_AT and not (isinstance(t, int) and t == LAST):
                        turn(t, *T_AT[c, s])
                for e in range(DB):
                    s = 2 * DB + e
                    wait(pe, gate_read, t * S_GATE + c * GATE + s - 2)
                    last = fold_part(g_bank[s % 3], H, e, True)
                last.then_inc(u_used, 1)
                pe.wait_ge(rs_lo, t * S_TWO + (c + 1) * TWO)
                for e in range(DB):
                    own_part(g_bank[(2 * DB + e) % 3], H, e, rs_c, True).then_inc(gate_done, 1)

            def own_part(b, g, e, v, last=False):
                for k in range(DB):
                    m = three(b[:, :], own[:, HI, k, g, e * P:(e + 1) * P], own[:, LO, k, g, e * P:(e + 1) * P],
                              v[:, HI, k, :], v[:, LO, k, :], k == 0 and not last, k == DB - 1 and last)
                return m

            def fold_part(b, g, e, first):
                for k in range(DB):
                    m = three(b[:, :], fold[:, HI, k, g, e * P:(e + 1) * P], fold[:, LO, k, g, e * P:(e + 1) * P],
                              u_c[:, HI, k, :], u_c[:, LO, k, :], k == 0 and first, k == DB - 1 and not first)
                return m

            def step(t, first=False):
                aggregate(t, 0, first)
                if first:
                    prepare()
                aggregate(t, 1, first)
                for c in range(NC):
                    gate_chunk(t, c)
                    if c + 2 < NC:
                        aggregate(t, c + 2, first)

            def turn_x():
                pe.wait_ge(const_ready, 2)
                pe.wait_ge(x_loaded, 16)
                for n in range(DB * NC):
                    d, c = n % DB, n // DB
                    for b in range(BC):
                        last = nc.tensor.transpose(bank[n][:, b * P:(b + 1) * P], x_raw[:, c * BC + b, d * P:(d + 1) * P], ident[:, :])
                    last.then_inc(x_turned, 1)
                pe.wait_ge(state0, DB * NC)

            def prepare():
                n = 0
                pe.wait_ge(w_loaded, 16 * (NG + 4))
                pe.wait_ge(small_loaded, 16 * N_SMALL)

                def bank_of(n):
                    wait(pe, prep_read, n - 2)
                    return g_bank[n % 3]

                for w in range(2):
                    b_ = bank_of(n)
                    for k in range(DB):
                        for b in range(DB):
                            last = nc.tensor.transpose(b_[:, (k * DB + b) * P:(k * DB + b + 1) * P],
                                                       o_raw[:, w, b, k * P:(k + 1) * P], ident[:, :])
                    last.then_inc(prep_done, 1)
                    n += 1
                for g in range(NG):
                    for k2 in range(NPREP_G):
                        b_ = bank_of(n)
                        for k in range(DB):
                            for b in range(DB):
                                kk = k2 * DB + k
                                last = nc.tensor.transpose(b_[:, (k * DB + b) * P:(k * DB + b + 1) * P],
                                                           gate_raw[g][:, b, kk * P:(kk + 1) * P], ident[:, :])
                        last.then_inc(prep_done, 1)
                        n += 1
                    b_ = bank_of(n)
                    wait(pe, prep_read, n)
                    for k in range(DB):
                        for m in range(2 * DB):
                            last = nc.tensor.matmul(b_[:, k * D:(k + 1) * D], lin_raw[:, m // DB, m % DB, k * P:(k + 1) * P],
                                                    gate_T[:, m, :], start=(m == 0), stop=(m == 2 * DB - 1))
                    last.then_inc(prep_done, 1)
                    n += 1
                    b_ = bank_of(n)
                    for e in range(DB):
                        for m in range(2 * DB):
                            last = nc.tensor.matmul(b_[:, e:e + 1], gate_T[:, m, e * P:(e + 1) * P],
                                                    bias[:, NG + 1 + m // DB, m % DB:m % DB + 1],
                                                    start=(m == 0), stop=(m == 2 * DB - 1))
                    last.then_inc(prep_done, 1)
                    n += 1
                pe.wait_ge(prep_read, n)

            def count_odd():
                pe.wait_ge(odd_ready, 1)
                nc.tensor.matmul(t_bank[0:1, 0:1], odd[:, 2:3], ones[:, 0:1], start=True, stop=True).then_inc(odd_done, 1)

            def hidden(c):
                v = (st_c, u_c)[c % 2]
                pe.wait_ge(st_lo, N_STEPS * S_TWO + (c + 1) * TWO)
                for e in range(DB):
                    wait(pe, hid_act, (c - 1) * DB + e + 1)
                    for k in range(DB):
                        last = three(u_bank[e][:, :], o_w[:, HI, 0, k, e * P:(e + 1) * P], o_w[:, LO, 0, k, e * P:(e + 1) * P],
                                     v[:, HI, k, :], v[:, LO, k, :], k == 0, k == DB - 1)
                    last.then_inc(hid_done, 1)

            def output(c):
                pe.wait_ge(hid_lo, (c + 1) * DB)
                v = hid_c[c % 2]
                if c == 0:
                    pe.wait_ge(gate_read, N_STEPS * S_GATE)
                for b in range(BC):
                    wait(pe, o_read, (c - 1) * BC + b + 1)
                    for k in range(DB):
                        last = three(out_bank[b][:, 0:D], v[HI][:, k, b * P:(b + 1) * P], v[LO][:, k, b * P:(b + 1) * P], o_w[:, HI, 1, k, :], o_w[:, LO, 1, k, :],
                                     k == 0, k == DB - 1)
                    last.then_inc(o_done, 1)

            turn_x()
            pe.wait_ge(ones_ready, 1)
            step(0, first=True)
            with pe.Fori(1, LAST) as t:
                step(t)
            aggregate(LAST, 0)
            aggregate(LAST, 1)
            count_odd()
            for c in range(NC):
                gate_chunk(LAST, c)
                if c + 2 < NC:
                    aggregate(LAST, c + 2)
            hidden(0)
            for c in range(NC):
                if c + 1 < NC:
                    hidden(c + 1)
                output(c)

        @block.scalar
        def _(act):
            def high(out_, in_, s):
                nc.scalar.activation(out_, in_, ACT.Copy).then_inc(s, 1)

            def expand_staged(c, p):
                q = c * NP + p
                wait(act, pair_used, q + 1 - RING)
                act.wait_ge(stage_loaded[q % STAGES], 16 * (q // STAGES + 1))
                high(ring[:, p % RING], stage[:, q % STAGES], pair_ready)

            def split_u(t, c, d):
                if d == 0:
                    act.wait_ge(agg_done, t * NC + c + 1)
                else:
                    act.wait_ge(pair_used, t * S_PAIR + (c + 1) * NP)
                wait(act, u_used, t * NC + c)
                high(u_c[:, HI, d, :], u_bank[2 * (c % 2) + d][:, :], u_hi)

            def split_state(t, c, e):
                if not (isinstance(t, int) and t == 0):
                    act.wait_ge(state_new, (t - 1) * S_TWO + c * TWO + e + 1)
                wait(act, gate_done, t * S_GATE + (c - 1) * GATE + 2 * DB)
                high(st_c[:, HI, e, :], stateT[:, e, c * CW:(c + 1) * CW], st_hi)

            def row_high(t, k, h):
                act.wait_ge(turn_done, t * S_TWO + 2 * k + h + 1)
                b = k * BC + 2 * h
                high(rows[:, HI, b:b + 2, :].rearrange("p b d -> p (b d)"), t_bank[:, :], row_hi)

            def gate(t, c, s):
                act.wait_ge(gate_read, t * S_GATE + c * GATE + s + 1)
                g, e = s // DB, s % DB
                nc.scalar.activation(gates[:, g, e, :], gates[:, g, e, :], ACT.Tanh if g == H else ACT.Sigmoid,
                                     bias=bias[:, g, e:e + 1]).then_inc(gate_act, 1)

            def rs_high(t, c, e):
                wait(act, gate_done, t * S_GATE + c * GATE)
                act.wait_ge(rs_ready, t * S_TWO + c * TWO + e + 1)
                high(rs_c[:, HI, e, :], tmp[:, e, :], rs_hi)

            def gate_chunk(t, c, first, last):
                for s in range(GATE):
                    gate(t, c, s)
                    if (c, s) in T_AT and not last:
                        row_high(t, *T_AT[c, s])
                    if s < DB:
                        rs_high(t, c, s)
                        continue
                    if first and c + 2 < NC and s < 2 * DB:
                        expand_staged(c + 2, 2 * (s - DB))
                        expand_staged(c + 2, 2 * (s - DB) + 1)
                    if c == NC - 2 and s == 2 * DB - 1:
                        for e in range(DB):
                            split_state(t, NC - 1, e)
                        for d in range(DB):
                            split_u(t, NC - 1, d)

            def aggregate(t, c, first):
                for n in range(2 * DB):
                    if first:
                        expand_staged(c, LEAD + n)
                    if n < DB:
                        split_u(t, c - 1, n)
                    else:
                        split_state(t, c - 1, n - DB)

            def step(t, first=False, last=False):
                if first:
                    for p in range(NP):
                        expand_staged(0, p)
                    for p in range(LEAD):
                        expand_staged(1, p)
                    prepare()
                else:
                    for h in range(2):
                        row_high(t - 1, NC - 1, h)
                aggregate(t, 1, first)
                for c in range(NC):
                    gate_chunk(t, c, first, last)
                    if c + 2 < NC:
                        aggregate(t, c + 2, first)

            def prepare():
                n = 0
                for w in range(2):
                    act.wait_ge(prep_done, n + 1)
                    high(o_w[:, HI, w].rearrange("p k d -> p (k d)"), g_bank[n % 3][:, :], prep_hi)
                    n += 1
                for g in range(NG):
                    n += NPREP_G - 1
                    for dst in (own, fold):
                        act.wait_ge(prep_done, n + 1)
                        high(dst[:, HI, :, g, :], g_bank[n % 3][:, :].rearrange("p (k d) -> p k d", d=D), prep_hi)
                        n += 1
                    n += 1

            act.wait_ge(x_loaded, 16)
            for c in range(NC):
                high(rows[:, HI, c * BC:(c + 1) * BC, :], x_raw[:, c * BC:(c + 1) * BC, :], x_hi)

            step(0, first=True)
            with act.Fori(1, LAST) as t:
                step(t)
            step(LAST, last=True)

            def final_split(c):
                v = (st_c, u_c)[c % 2]
                wait(act, hid_done, (c - 1) * DB)
                for e in range(DB):
                    act.wait_ge(state_new, LAST * S_TWO + c * TWO + e + 1)
                    high(v[:, HI, e, :], stateT[:, e, c * CW:(c + 1) * CW], st_hi)

            act.wait_ge(gate_done, N_STEPS * S_GATE)
            final_split(0)
            final_split(1)
            for c in range(NC):
                for e in range(DB):
                    act.wait_ge(hid_done, c * DB + e + 1)
                    wait(act, hid_lo, (c - 1) * DB + e + 1)
                    nc.scalar.activation(hid[:, e, :], u_bank[e][:, :], ACT.Tanh, bias=bias[:, NG, e:e + 1]).then_inc(hid_act, 1)
                for e in range(DB):
                    act.wait_ge(hid_act, c * DB + e + 1)
                    wait(act, o_done, (c - 1) * BC)
                    high(hid_c[c % 2][HI][:, e, :], hid[:, e, :], hid_hi)
                if c + 2 < NC:
                    final_split(c + 2)
            nc.scalar.activation(std[:, 0:1], ones[:, 0:1], ACT.Sqrt).then_inc(std_first, 1)
            act.wait_ge(var_ready, 1)
            act.wait_ge(std_first, 1)
            nc.scalar.activation(std[:, :], mv[:, :, 1], ACT.Sqrt).then_inc(std_ready, 1)
            act.wait_ge(shift_ready, 1)
            for c in range(NC):
                last = nc.scalar.activation(y[:, (c + 1) * BC - 1, :], y[:, (c + 1) * BC - 1, :], ACT.Identity,
                                            scale=rstd[:, (c + 1) * BC - 1:(c + 1) * BC],
                                            bias=shift[:, (c + 1) * BC - 1:(c + 1) * BC])
                last.then_inc(y_last, 1)

        @block.vector
        def _(dve):
            def low(out_, in_, hi_, s):
                nc.vector.tensor_tensor(out_, in_, hi_.bitcast(F32), ALU.subtract).then_inc(s, 1)

            def expand(t, c, p):
                wait(dve, pair_used, t * S_PAIR + c * NP + p + 1 - RING)
                nc.vector.tensor_copy(ring[:, p % RING], a8[:, c, 2 * p:2 * p + 2, :]).then_inc(pair_ready, 1)

            def store_pair(c, p):
                q = c * NP + p
                dve.wait_ge(stage_loaded[q % STAGES], 16 * (q // STAGES + 1))
                nc.vector.tensor_scalar(a8[:, c, 2 * p:2 * p + 2, :], stage[:, q % STAGES].bitcast(U32), 1.0, 0.0,
                                        ALU.mult, ALU.max, accum_out=above[:, q:q + 1]).then_inc(pair_stored, 1)

            def check(c, p):
                for h in range(2):
                    if (c, p, h) not in checks:
                        continue
                    n = checks.index((c, p, h))
                    dve.wait_ge(check_done, n + 1)
                    off = (2 * p % BC) * P
                    b = c * BC + 2 * h
                    dve.wait_ge(pair_stored, (2 * p // BC) * NP + b // 2 + 1)
                    wait(dve, check_read, n)
                    nc.vector.scalar_tensor_tensor(
                        out=differs[:, :, :], in0=check_bank[n % 2][:, :].rearrange("p (b j) -> p b j", b=2), scalar=1.0,
                        in1=a8[:, 2 * p // BC, b:b + 2, off:off + 2 * P], op0=ALU.mult, op1=ALU.not_equal,
                        accum_out=differ[:, n:n + 1]).then_inc(check_read, 1)

            def pair(t, c, p, first):
                if first:
                    store_pair(c, p)
                else:
                    expand(t, c, p)

            def split_u(t, c, d):
                dve.wait_ge(u_hi, t * S_TWO + c * TWO + d + 1)
                low(u_c[:, LO, d, :], u_bank[2 * (c % 2) + d][:, :], u_c[:, HI, d, :], u_lo)

            def split_state(t, c, e):
                dve.wait_ge(st_hi, t * S_TWO + c * TWO + e + 1)
                low(st_c[:, LO, e, :], stateT[:, e, c * CW:(c + 1) * CW], st_c[:, HI, e, :], st_lo)

            def row_low(t, k, h):
                dve.wait_ge(row_hi, t * S_TWO + 2 * k + h + 1)
                b = k * BC + 2 * h
                low(rows[:, LO, b:b + 2, :].rearrange("p b d -> p (b d)"), t_bank[:, :],
                    rows[:, HI, b:b + 2, :].rearrange("p b d -> p (b d)"), row_lo)

            def gate(t, c, s):
                g, e = s // DB, s % DB
                dve.wait_ge(gate_done, t * S_GATE + c * GATE + s + 1)
                nc.vector.scalar_tensor_tensor(out=gates[:, g, e, :], in0=degree[:, c * CW:(c + 1) * CW],
                                               scalar=deg_w[:, g, e:e + 1], in1=g_bank[s % 3][:, :],
                                               op0=ALU.mult, op1=ALU.add).then_inc(gate_read, 1)

            def rs(t, c, e):
                dve.wait_ge(gate_act, t * S_GATE + c * GATE + e + 1)
                nc.vector.tensor_tensor(tmp[:, e, :], gates[:, R, e, :], stateT[:, e, c * CW:(c + 1) * CW],
                                        ALU.mult).then_inc(rs_ready, 1)

            def rs_low(t, c, e):
                dve.wait_ge(rs_hi, t * S_TWO + c * TWO + e + 1)
                low(rs_c[:, LO, e, :], tmp[:, e, :], rs_c[:, HI, e, :], rs_lo)

            def update(t, c, e):
                old = stateT[:, e, c * CW:(c + 1) * CW]
                n = 2 * (t * S_TWO + c * TWO + e)
                dve.wait_ge(gate_act, t * S_GATE + c * GATE + H * DB + e + 1)
                nc.vector.tensor_tensor(tmp[:, e, :], gates[:, H, e, :], old, ALU.subtract).then_inc(chain, 1)
                dve.wait_ge(chain, n + 1)
                nc.vector.tensor_tensor(tmp[:, e, :], tmp[:, e, :], gates[:, Z, e, :], ALU.mult).then_inc(chain, 1)
                dve.wait_ge(chain, n + 2)
                nc.vector.tensor_tensor(old, old, tmp[:, e, :], ALU.add).then_inc(state_new, 1)

            def gate_chunk(t, c, first, last):
                if c + 2 < NC:
                    ahead = (t, c + 2, first)
                elif c == NC - 2 and not last:
                    ahead = (t + 1, 0, False)
                else:
                    ahead = None

                def next_pair(p):
                    if ahead:
                        pair(ahead[0], ahead[1], p, ahead[2])

                def turned(s):
                    if (c, s) in T_AT and not last:
                        row_low(t, *T_AT[c, s])

                if c == NC - 1:
                    update(t, c - 1, 0)
                gate(t, c, 0)
                turned(0)
                next_pair(0)
                rs(t, c, 0)
                if c == NC - 1:
                    update(t, c - 1, 1)
                gate(t, c, 1)
                turned(1)
                rs_low(t, c, 0)
                rs(t, c, 1)
                next_pair(1)
                gate(t, c, 2)
                turned(2)
                rs_low(t, c, 1)
                next_pair(2)
                gate(t, c, 3)
                turned(3)
                next_pair(3)
                if c == NC - 2:
                    for e in range(DB):
                        split_state(t, NC - 1, e)
                    for d in range(DB):
                        split_u(t, NC - 1, d)
                gate(t, c, 4)
                gate(t, c, 5)

            def aggregate(t, c, first):
                for n in range(2 * DB):
                    if c >= 2 and n < DB:
                        update(t, c - 2, n)
                    pair(t, c, LEAD + n, first)
                    if first:
                        check(c, n)
                    if n < DB:
                        split_u(t, c - 1, n)
                    else:
                        split_state(t, c - 1, n - DB)
                if first:
                    for p in range(LEAD, NP):
                        check(c, p)
                    degrees(c)

            def degrees(c):
                dve.wait_ge(pair_used, (c + 1) * NP)
                nc.vector.tensor_copy(degree[:, c * CW:(c + 1) * CW], g_bank[0][:, :]).then_inc(degree_read, 1)

            def step(t, first=False, last=False):
                if first:
                    for p in range(NP):
                        store_pair(0, p)
                        check(0, p)
                    for p in range(LEAD):
                        store_pair(1, p)
                    degrees(0)
                    prepare()
                else:
                    update(t - 1, NC - 1, 0)
                    expand(t, 0, 4)
                    update(t - 1, NC - 1, 1)
                    expand(t, 0, 5)
                    row_low(t - 1, NC - 1, 0)
                    expand(t, 0, 6)
                    row_low(t - 1, NC - 1, 1)
                    expand(t, 0, 7)
                    for p in range(LEAD):
                        expand(t, 1, p)
                aggregate(t, 1, first)
                if last:
                    odd_count()
                for c in range(NC):
                    gate_chunk(t, c, first, last)
                    if c + 2 < NC:
                        aggregate(t, c + 2, first)

            def prepare():
                n = 0
                hi = 0
                for w in range(2):
                    dve.wait_ge(prep_hi, hi + 1)
                    low(o_w[:, LO, w].rearrange("p k d -> p (k d)"), g_bank[n % 3][:, :],
                        o_w[:, HI, w].rearrange("p k d -> p (k d)"), prep_read)
                    n, hi = n + 1, hi + 1
                for g in range(NG):
                    for k2 in range(NPREP_G - 1):
                        dve.wait_ge(prep_done, n + 1)
                        nc.vector.tensor_copy(gate_T[:, k2 * DB:(k2 + 1) * DB, :].rearrange("p k d -> p (k d)"),
                                              g_bank[n % 3][:, :]).then_inc(prep_read, 1)
                        n += 1
                    for dst in (own, fold):
                        dve.wait_ge(prep_hi, hi + 1)
                        low(dst[:, LO, :, g, :], g_bank[n % 3][:, :].rearrange("p (k d) -> p k d", d=D),
                            dst[:, HI, :, g, :], prep_read)
                        n, hi = n + 1, hi + 1
                    dve.wait_ge(prep_done, n + 1)
                    nc.vector.tensor_copy(deg_w[:, g, :], g_bank[n % 3][:, 0:DB]).then_inc(prep_read, 1)
                    n += 1

            def odd_count():
                nc.vector.tensor_scalar(above[:, :], above[:, :], 1.0, 0.0, ALU.is_gt, ALU.add,
                                        accum_out=odd[:, 0:1]).then_inc(fin_link, 1)
                nc.vector.tensor_scalar(differ[:, :], differ[:, :], 1.0, 0.0, ALU.mult, ALU.add,
                                        accum_out=odd[:, 1:2]).then_inc(fin_link, 1)
                dve.wait_ge(fin_link, 2)
                nc.vector.tensor_tensor(odd[:, 2:3], odd[:, 0:1], odd[:, 1:2], ALU.add).then_inc(odd_ready, 1)
                dve.wait_ge(odd_done, 1)
                nc.vector.tensor_copy(flag, t_bank[0:1, 0:1]).then_inc(fin_link, 1)

            dve.wait_ge(const_ready, 2)
            nc.vector.tensor_copy(ones_r[:, :], ones[:, :]).then_inc(ones_ready, 1)
            for c in range(NC):
                dve.wait_ge(x_hi, c + 1)
                low(rows[:, LO, c * BC:(c + 1) * BC, :], x_raw[:, c * BC:(c + 1) * BC, :],
                    rows[:, HI, c * BC:(c + 1) * BC, :], x_split)
            for n in range(DB * NC):
                d, c = n % DB, n // DB
                dve.wait_ge(x_turned, n + 1)
                nc.vector.tensor_copy(stateT[:, d, c * CW:(c + 1) * CW], bank[n][:, :]).then_inc(state0, 1)
            step(0, first=True)
            with dve.Fori(1, LAST) as t:
                step(t)
            step(LAST, last=True)

            def final_split(c):
                v = (st_c, u_c)[c % 2]
                for e in range(DB):
                    dve.wait_ge(st_hi, N_STEPS * S_TWO + c * TWO + e + 1)
                    low(v[:, LO, e, :], stateT[:, e, c * CW:(c + 1) * CW], v[:, HI, e, :], st_lo)

            def split_hidden(c):
                for e in range(DB):
                    dve.wait_ge(hid_hi, c * DB + e + 1)
                    low(hid_c[c % 2][LO][:, e, :], hid[:, e, :], hid_c[c % 2][HI][:, e, :], hid_lo)

            def mean_and_variance(c):
                dve.wait_ge(residual_ready, c + 1)
                for b in range(BC):
                    n = c * BC + b
                    dve.wait_ge(o_done, n + 1)
                    nc.vector.tensor_tensor(y[:, n, :], out_bank[b][:, 0:D], x_res[:, n, :], ALU.add).then_inc(o_read, 1)
                for n in range(c * BC, (c + 1) * BC):
                    dve.wait_ge(o_read, n + 1)
                    nc.vector.bn_stats(stats[:, n, :], y[:, n, :]).then_inc(stats_ready, 1)
                for n in range(c * BC, (c + 1) * BC):
                    dve.wait_ge(stats_ready, n + 1)
                    nc.vector.bn_aggr(mv[:, n, :], stats[:, n, :]).then_inc(aggr_ready, 1)

            final_split(0)
            for e in range(DB):
                update(LAST, NC - 1, e)
            final_split(1)
            for c in range(NC):
                split_hidden(c)
                if c + 2 < NC:
                    final_split(c + 2)
                if c:
                    mean_and_variance(c - 1)
            mean_and_variance(NC - 1)
            dve.wait_ge(aggr_ready, NB)
            nc.vector.tensor_scalar(mv[:, :, 1], mv[:, :, 1], EPS, None, ALU.add).then_inc(var_ready, 1)
            dve.wait_ge(std_ready, 1)
            nc.vector.reciprocal(rstd[:, :], std[:, :]).then_inc(fin_link, 1)
            dve.wait_ge(fin_link, 4)
            nc.vector.scalar_tensor_tensor(out=shift[:, :], in0=mv[:, :, 0], scalar=-1.0, in1=rstd[:, :],
                                           op0=ALU.mult, op1=ALU.mult).then_inc(shift_ready, 1)
            for c in range(NC):
                for b in range(BC - 1):
                    n = c * BC + b
                    last = nc.vector.tensor_scalar(y[:, n, :], y[:, n, :], mv[:, n, 0:1], rstd[:, n:n + 1],
                                                   ALU.subtract, ALU.mult)
                last.then_inc(y_ready, 1)


def general_path(nc, flag, x, adj, in_W, in_b, out_W, out_b, r_W, r_b, z_W, z_b, h_W, h_b,
                 o1_W, o1_b, o2_W, o2_b, out):
    N, D = x.shape
    NB = N // P
    NC = N // CW
    DB = D // P
    BC = CW // P
    NG = 3
    KB = NG * DB
    R, Z, H = range(NG)

    with ExitStack() as ctx:
        def sb(name, shape, dt=F32):
            return ctx.enter_context(nc.sbuf_tensor("g_" + name, shape, dt))

        def pb(name, shape, dt=F32):
            return ctx.enter_context(nc.psum_tensor("g_" + name, shape, dt))

        def sem(name):
            return ctx.enter_context(nc.semaphore("g_" + name))

        a_dram = nc.dram_tensor("a_dram", [N, N], F32, kind="Internal").ap()
        at_dram = nc.dram_tensor("at_dram", [N, N], F32, kind="Internal").ap()

        ident = sb("ident", [P, P])
        xb = sb("xb", [P, NB, D])
        stateT = sb("stateT", [P, DB, N])
        lin_raw = sb("lin_raw", [P, 4, DB, D])
        lin_T = sb("lin_T", [P, 4, DB, D])
        gate_raw = sb("gate_raw", [P, DB, NG * D])
        gate_T = sb("gate_T", [P, NG, KB, D])
        gate_b = sb("gate_b", [P, NG, DB])
        o1_bc = sb("o1_bc", [P, DB])
        io_b = sb("io_b", [P, 2 * D])
        o2_bb = sb("o2_bb", [P, D])
        s_io = sb("s_io", [P, NB, 2 * D])
        a_io = sb("a_io", [P, 4, CW])
        gates = sb("gates", [P, NG, DB, CW])
        rs = sb("rs", [P, DB, CW])
        tmp = sb("tmp", [P, DB, CW])
        tile = sb("tile", [P, 2, 2, 2, CW])
        y = sb("y", [P, BC, D])
        stats = sb("stats", [P, BC, 6])
        mv = sb("mv", [P, BC, 2])
        rstd = sb("rstd", [P, BC])
        araw = s_io[:, 0:4, :].bitcast(I32)
        af = s_io[:, 4:8, :]
        att = s_io[:, 8:12, :]

        bank = [pb(f"bank{i}", [P, CW]) for i in range(8)]

        loaded = sem("loaded")
        ident_zeroed = sem("ident_zeroed")
        ident_ready = sem("ident_ready")
        prep_done = sem("prep_done")
        prep_copied = sem("prep_copied")
        gate_loaded = sem("gate_loaded")
        gate_used = sem("gate_used")
        xb_ready = sem("xb_ready")
        araw_loaded = sem("araw_loaded")
        af_ready = sem("af_ready")
        at_done = sem("at_done")
        att_ready = sem("att_ready")
        a_stored = sem("a_stored")
        proj_done = sem("proj_done")
        proj_read = sem("proj_read")
        tile_loaded = [sem(f"tile_loaded{i}") for i in range(2)]
        tile_used = sem("tile_used")
        agg_done = sem("agg_done")
        agg_read = sem("agg_read")
        gate_done = sem("gate_done")
        gate_read = sem("gate_read")
        rs_ready = sem("rs_ready")
        link = sem("link")
        state_ready = sem("state_ready")
        hid_done = sem("hid_done")
        hid_ready = sem("hid_ready")
        o_done = sem("o_done")
        o_read = sem("o_read")
        var_ready = sem("var_ready")
        std_ready = sem("std_ready")
        y_ready = sem("y_ready")
        y_stored = sem("y_stored")

        block = ctx.enter_context(nc.Block())

        LOADS = 4 + 3 * 1 + 1 + 2 + 1 + 1
        NLIN = 4 * DB
        x_v = x.rearrange("(b p) d -> p b d", p=P)

        @block.sync
        def _(sp):
            with sp.If(sp.value_load(flag, min_val=0, max_val=MISMATCHES) != 0):
                for n, w in enumerate((in_W, out_W, o1_W, o2_W)):
                    sp.dma_start(lin_raw[:, n], w.rearrange("(b p) k -> p b k", p=P)).then_inc(loaded, 16)
                for g, b in enumerate((r_b, z_b, h_b)):
                    sp.dma_start(gate_b[:, g], b.rearrange("(b p) -> p b", p=P), allow_slow_non_contiguous=True).then_inc(loaded, 16)
                sp.dma_start(o1_bc[:, :], o1_b.rearrange("(b p) -> p b", p=P), allow_slow_non_contiguous=True).then_inc(loaded, 16)
                sp.dma_start(io_b[:, 0:D], in_b.partition_broadcast(P)).then_inc(loaded, 16)
                sp.dma_start(io_b[:, D:], out_b.partition_broadcast(P)).then_inc(loaded, 16)
                sp.dma_start(o2_bb[:, :], o2_b.partition_broadcast(P)).then_inc(loaded, 16)
                sp.dma_start(xb[:, :, :], x_v).then_inc(loaded, 16)
                for g, w in enumerate((r_W, z_W, h_W)):
                    if g:
                        sp.wait_ge(gate_used, g)
                    sp.dma_start(gate_raw[:, :, :], w.rearrange("(b p) k -> p b k", p=P)).then_inc(gate_loaded, 16)
                with sp.Fori(0, NB) as b:
                    column = sp.snap(b * P)
                    sp.wait_ge(a_stored, 1 + b * 32)
                    sp.dma_start(araw, adj[bass.ds(b * P, P), :].rearrange("p (c w) -> p c w", c=NC)).then_inc(araw_loaded, 16)
                    sp.wait_ge(att_ready, 1 + (b + 1) * NC)
                    sp.dma_start(a_dram[bass.ds(b * P, P), :].rearrange("p (c w) -> p c w", c=NC), af).then_inc(a_stored, 16)
                    sp.dma_start(at_dram[:, bass.ds(column, P)].rearrange("(j p) i -> p j i", p=P),
                                 att.rearrange("p c (j i) -> p (c j) i", i=P)).then_inc(a_stored, 16)
                sp.wait_ge(a_stored, 1 + NB * 32)
                a_v = a_dram.rearrange("(j p) i -> p j i", p=P)
                at_v = at_dram.rearrange("(j p) i -> p j i", p=P)
                with sp.Fori(0, N_STEPS * NC) as q:
                    col = sp.snap((q % NC) * CW)
                    for j in range(NB // 2):
                        n = q * (NB // 2) + j
                        if j >= 2:
                            sp.wait_ge(tile_used, 1 + n - 1)
                        else:
                            sp.wait_ge(tile_used, 1 + q * (NB // 2))
                        for m, v in enumerate((at_v, a_v)):
                            sp.dma_start(tile[:, j % 2, m], v[:, 2 * j:2 * j + 2, bass.ds(col, CW)])\
                              .then_inc(tile_loaded[j % 2], 16)
                with sp.Fori(0, NC) as c:
                    sp.wait_ge(y_ready, (c + 1) * BC)
                    sp.dma_start(out.rearrange("(b p) d -> p b d", p=P)[:, bass.ds(c * BC, BC), :], y[:, :, :]).then_inc(y_stored, 16)
                sp.wait_ge(y_stored, 16 * NC)

        @block.gpsimd
        def _(pool):
            with pool.If(pool.value_load(flag, min_val=0, max_val=MISMATCHES) != 0):
                for s in (a_stored, tile_used, att_ready, state_ready, agg_read, gate_read, hid_ready, o_read, o_done):
                    pool.sem_inc(s, 1)
                nc.gpsimd.memset(ident[:, :], 0.0).then_inc(ident_zeroed, 1)
                pool.wait_ge(ident_zeroed, 1)
                nc.gpsimd.affine_select(out=ident[:, :], in_=ident[:, :], compare_op=ALU.not_equal, fill=1.0,
                                        base=0, pattern=[[-1, P]], channel_multiplier=1).then_inc(ident_ready, 1)

        @block.tensor
        def _(pe):
            with pe.If(pe.value_load(flag, min_val=0, max_val=MISMATCHES) != 0):
                pe.wait_ge(ident_ready, 1)
                pe.wait_ge(loaded, 16 * LOADS)
                n = 0
                for w in range(4):
                    for k in range(DB):
                        if n >= 8:
                            pe.wait_ge(prep_copied, n - 7)
                        for b in range(DB):
                            last = nc.tensor.transpose(bank[n % 8][:, b * P:(b + 1) * P], lin_raw[:, w, b, k * P:(k + 1) * P], ident[:, :])
                        last.then_inc(prep_done, 1)
                        n += 1
                for g in range(NG):
                    pe.wait_ge(gate_loaded, 16 * (g + 1))
                    for k in range(KB):
                        if n >= 8:
                            pe.wait_ge(prep_copied, n - 7)
                        for b in range(DB):
                            last = nc.tensor.transpose(bank[n % 8][:, b * P:(b + 1) * P], gate_raw[:, b, k * P:(k + 1) * P], ident[:, :])
                        last.then_inc(prep_done, 1)
                        n += 1
                for d in range(DB):
                    for c in range(NC):
                        pe.wait_ge(prep_copied, n - 7)
                        for b in range(BC):
                            last = nc.tensor.transpose(bank[n % 8][:, b * P:(b + 1) * P], xb[:, c * BC + b, d * P:(d + 1) * P], ident[:, :])
                        last.then_inc(prep_done, 1)
                        n += 1
                pe.wait_ge(prep_copied, n)
                with pe.Fori(0, NB) as b:
                    pe.wait_ge(af_ready, b + 1)
                    pe.wait_ge(att_ready, 1 + b * NC)
                    for c in range(NC):
                        for j in range(BC):
                            last = nc.tensor.transpose(bank[c][:, j * P:(j + 1) * P], af[:, c, j * P:(j + 1) * P], ident[:, :])
                        last.then_inc(at_done, 1)
                pe.wait_ge(att_ready, 1 + NB * NC)
                pe.wait_ge(a_stored, 1 + NB * 32)
                with pe.Fori(0, N_STEPS) as t:
                    pe.wait_ge(state_ready, 1 + t * NC * DB)
                    for b in range(NB):
                        if b >= 2:
                            pe.wait_ge(proj_read, t * NB + b - 1)
                        for k in range(DB):
                            last = nc.tensor.matmul(bank[b % 2][:, :], stateT[:, k, b * P:(b + 1) * P],
                                                    lin_T[:, 0:2, k, :], start=(k == 0), stop=(k == DB - 1))
                        last.then_inc(proj_done, 1)
                    with pe.Fori(0, NC) as c:
                        q = t * NC + c
                        pe.wait_ge(proj_read, (t + 1) * NB)
                        pe.wait_ge(agg_read, 1 + 4 * q)
                        for j in range(NB):
                            if j % 2 == 0:
                                pe.wait_ge(tile_loaded[j // 2 % 2], 32 * (q * (NB // 4) + j // 4 + 1))
                            for m in range(2):
                                for d in range(DB):
                                    last = nc.tensor.matmul(bank[2 + m * DB + d][:, :],
                                                            s_io[:, j, m * D + d * P:m * D + (d + 1) * P],
                                                            tile[:, j // 2 % 2, m, j % 2, :],
                                                            start=(j == 0), stop=(j == NB - 1))
                            if j == NB - 1:
                                last.then_inc(agg_done, 1)
                            if j % 2 == 1:
                                if j == NB - 1:
                                    pe.wait_ge(agg_done, q + 1)
                                    pe.sem_inc(tile_used, 1)
                                else:
                                    last.then_inc(tile_used, 1)
                        pe.wait_ge(agg_read, 1 + 4 * (q + 1))
                        for s in range(NG * DB):
                            g, e = s // DB, s % DB
                            pe.wait_ge(gate_read, 1 + q * NG * DB + (s - 1 if s >= 2 else 0))
                            for k in range(KB):
                                if k < 4:
                                    rhs = a_io[:, k, :]
                                elif g == H:
                                    if k == 4:
                                        pe.wait_ge(rs_ready, (q + 1) * DB)
                                    rhs = rs[:, k - 4, :]
                                else:
                                    rhs = stateT[:, k - 4, bass.ds(c * CW, CW)]
                                last = nc.tensor.matmul(bank[6 + s % 2][:, :], gate_T[:, g, k, e * P:(e + 1) * P], rhs,
                                                        start=(k == 0), stop=(k == KB - 1))
                            last.then_inc(gate_done, 1)
                pe.wait_ge(state_ready, 1 + N_STEPS * NC * DB)
                pe.wait_ge(gate_read, 1 + N_STEPS * NC * NG * DB)
                with pe.Fori(0, NC) as c:
                    pe.wait_ge(hid_ready, 1 + c * DB)
                    for e in range(DB):
                        for k in range(DB):
                            last = nc.tensor.matmul(bank[e][:, :], lin_T[:, 2, k, e * P:(e + 1) * P],
                                                    stateT[:, k, bass.ds(c * CW, CW)], start=(k == 0), stop=(k == DB - 1))
                        last.then_inc(hid_done, 1)
                    pe.wait_ge(hid_ready, 1 + (c + 1) * DB)
                    pe.wait_ge(o_read, 1 + c * BC)
                    for b in range(BC):
                        for k in range(DB):
                            last = nc.tensor.matmul(bank[2 + b][:, 0:D], rs[:, k, b * P:(b + 1) * P],
                                                    lin_T[:, 3, k, :], start=(k == 0), stop=(k == DB - 1))
                        last.then_inc(o_done, 1)

        @block.scalar
        def _(act):
            with act.If(act.value_load(flag, min_val=0, max_val=MISMATCHES) != 0):
                with act.Fori(0, N_STEPS * NC) as q:
                    act.wait_ge(state_ready, 1 + q * DB)
                    for s in range(NG * DB):
                        g, e = s // DB, s % DB
                        act.wait_ge(gate_done, q * NG * DB + s + 1)
                        nc.scalar.activation(gates[:, g, e, :], bank[6 + s % 2][:, :], ACT.Tanh if g == H else ACT.Sigmoid,
                                             bias=gate_b[:, g, e:e + 1]).then_inc(gate_read, 1)
                with act.Fori(0, NC) as c:
                    act.wait_ge(o_done, 1 + c * BC)
                    for e in range(DB):
                        act.wait_ge(hid_done, c * DB + e + 1)
                        nc.scalar.activation(rs[:, e, :], bank[e][:, :], ACT.Tanh, bias=o1_bc[:, e:e + 1]).then_inc(hid_ready, 1)
                    act.wait_ge(var_ready, c + 1)
                    nc.scalar.activation(rstd[:, :], mv[:, :, 1], ACT.Sqrt).then_inc(std_ready, 1)

        @block.vector
        def _(dve):
            with dve.If(dve.value_load(flag, min_val=0, max_val=MISMATCHES) != 0):
                n = 0
                for w in range(4):
                    for k in range(DB):
                        dve.wait_ge(prep_done, n + 1)
                        nc.vector.tensor_copy(lin_T[:, w, k, :], bank[n % 8][:, 0:D]).then_inc(prep_copied, 1)
                        n += 1
                for g in range(NG):
                    for k in range(KB):
                        dve.wait_ge(prep_done, n + 1)
                        if k == KB - 1:
                            dve.sem_inc(gate_used, 1)
                        nc.vector.tensor_copy(gate_T[:, g, k, :], bank[n % 8][:, 0:D]).then_inc(prep_copied, 1)
                        n += 1
                for d in range(DB):
                    for c in range(NC):
                        dve.wait_ge(prep_done, n + 1)
                        nc.vector.tensor_copy(stateT[:, d, c * CW:(c + 1) * CW], bank[n % 8][:, :]).then_inc(prep_copied, 1)
                        n += 1
                nc.vector.tensor_tensor(xb[:, :, :], xb[:, :, :], o2_bb[:, :].unsqueeze(1).broadcast_to([P, NB, D]), ALU.add).then_inc(xb_ready, 1)
                with dve.Fori(0, NB) as b:
                    dve.wait_ge(araw_loaded, 16 * (b + 1))
                    nc.vector.tensor_copy(af, araw).then_inc(af_ready, 1)
                    for c in range(NC):
                        dve.wait_ge(at_done, b * NC + c + 1)
                        nc.vector.tensor_copy(att[:, c, :], bank[c][:, :]).then_inc(att_ready, 1)
                dve.wait_ge(a_stored, 1 + NB * 32)
                with dve.Fori(0, N_STEPS) as t:
                    for b in range(NB):
                        dve.wait_ge(proj_done, t * NB + b + 1)
                        nc.vector.tensor_tensor(s_io[:, b, :], bank[b % 2][:, :], io_b[:, :], ALU.add).then_inc(proj_read, 1)
                    with dve.Fori(0, NC) as c:
                        q = t * NC + c
                        dve.wait_ge(agg_done, q + 1)
                        for k in range(4):
                            nc.vector.tensor_copy(a_io[:, k, :], bank[2 + k][:, :]).then_inc(agg_read, 1)
                        st = stateT[:, :, bass.ds(c * CW, CW)]
                        for e in range(DB):
                            dve.wait_ge(gate_read, 1 + q * NG * DB + e + 1)
                            nc.vector.tensor_tensor(rs[:, e, :], gates[:, R, e, :], stateT[:, e, bass.ds(c * CW, CW)], ALU.mult).then_inc(rs_ready, 1)
                        for e in range(DB):
                            se = stateT[:, e, bass.ds(c * CW, CW)]
                            u = 2 * (q * DB + e)
                            dve.wait_ge(gate_read, 1 + q * NG * DB + H * DB + e + 1)
                            nc.vector.tensor_tensor(tmp[:, e, :], gates[:, H, e, :], se, ALU.subtract).then_inc(link, 1)
                            dve.wait_ge(link, u + 1)
                            nc.vector.tensor_tensor(tmp[:, e, :], tmp[:, e, :], gates[:, Z, e, :], ALU.mult).then_inc(link, 1)
                            dve.wait_ge(link, u + 2)
                            nc.vector.tensor_tensor(se, se, tmp[:, e, :], ALU.add).then_inc(state_ready, 1)
                link0 = 2 * N_STEPS * NC * DB
                LN = 2 * BC + 1 + 2
                for c in range(NC):
                    if c:
                        dve.wait_ge(y_stored, 16 * c)
                    at = link0 + c * LN
                    for b in range(BC):
                        dve.wait_ge(o_done, 1 + c * BC + b + 1)
                        nc.vector.tensor_tensor(y[:, b, :], bank[2 + b][:, 0:D], xb[:, c * BC + b, :], ALU.add).then_inc(o_read, 1)
                    for b in range(BC):
                        dve.wait_ge(o_read, 1 + c * BC + b + 1)
                        nc.vector.bn_stats(stats[:, b, :], y[:, b, :]).then_inc(link, 1)
                    for b in range(BC):
                        dve.wait_ge(link, at + b + 1)
                        nc.vector.bn_aggr(mv[:, b, :], stats[:, b, :]).then_inc(link, 1)
                    dve.wait_ge(link, at + 2 * BC)
                    nc.vector.tensor_scalar(mv[:, :, 1], mv[:, :, 1], EPS, None, ALU.add).then_inc(var_ready, 1)
                    dve.wait_ge(std_ready, c + 1)
                    nc.vector.reciprocal(rstd[:, :], rstd[:, :]).then_inc(link, 3)
                    dve.wait_ge(link, at + 2 * BC + 3)
                    for b in range(BC):
                        nc.vector.tensor_scalar(y[:, b, :], y[:, b, :], mv[:, b, 0:1], rstd[:, b:b + 1], ALU.subtract, ALU.mult).then_inc(y_ready, 1)




def gnn_kernel(nc, *args):
    with nc.sbuf_tensor("flag", [1, 1], I32) as flag:
        fast_path(nc, flag[:, :], *args)
        general_path(nc, flag[:, :], *args)


_INS = ["x", "adj"] + ["L0_gnn_" + n for n in ("in_W", "in_b", "out_W", "out_b", "r_W", "r_b", "z_W", "z_b", "h_W", "h_b",
                                              "o1_W", "o1_b", "o2_W", "o2_b")]


def kernel(**inputs):
    import numpy as _np
    import concourse.bacc as _bacc
    from concourse import mybir as _mybir
    from concourse.bass_utils import run_bass_kernel_spmd as _run

    nc = _bacc.Bacc("TRN2", target_bir_lowering=False, num_devices=1)
    arrays, args = {}, []
    for name in _INS:
        a = _np.ascontiguousarray(inputs[name])
        arrays[f"in_{name}_dram"] = a
        args.append(nc.dram_tensor(f"in_{name}_dram", a.shape, _mybir.dt.from_np(a.dtype), kind="ExternalInput").ap())
    out = nc.dram_tensor("out_0_dram", inputs["x"].shape, _mybir.dt.float32, kind="ExternalOutput").ap()
    gnn_kernel(nc, *args, out)
    r = _run(nc, [arrays], core_ids=[0])
    return r.results[0]["out_0_dram"]
```

```python
from contextlib import ExitStack

import concourse.bass as bass
from concourse import mybir

F32 = mybir.dt.float32
F32R = mybir.dt.float32r
I32 = mybir.dt.int32
U32 = mybir.dt.uint32
U16 = mybir.dt.uint16
U8 = mybir.dt.uint8
ALU = mybir.AluOpType
ACT = mybir.ActivationFunctionType

P = 128
CW = 512
EPS = 1e-5
N_STEPS = 5
MISMATCHES = 1 << 23


def wait(eng, sem, value):
    if not isinstance(value, int) or value > 0:
        eng.wait_ge(sem, value)


def fast_path(nc, flag, x, adj, in_W, in_b, out_W, out_b, r_W, r_b, z_W, z_b, h_W, h_b,
              o1_W, o1_b, o2_W, o2_b, out):
    N, D = x.shape
    NB, NC, DB = N // P, N // CW, D // P
    BC = CW // P
    NG = 3
    R, Z, H = range(NG)
    HI, LO = range(2)
    NP = NB // 2
    RING, STAGES = 4, 3
    LEAD = RING
    LAST = N_STEPS - 1
    WARM_UP = 7

    S_GATE = NC * NG * DB
    GATE = NG * DB
    S_TWO, TWO = NC * DB, DB
    S_PAIR = NC * NP

    T_AT = {(2, 0): (0, 0), (2, 1): (0, 1), (2, 2): (1, 0), (2, 3): (1, 1), (3, 2): (2, 0), (3, 3): (2, 1)}

    FINAL_AT = {(2, 1): 0, (2, 2): 1, (3, 2): 2}

    with ExitStack() as ctx:
        def sb(name, shape, dt=F32):
            return ctx.enter_context(nc.sbuf_tensor(name, shape, dt))

        def sem(name):
            return ctx.enter_context(nc.semaphore(name))

        ident = sb("ident", [P, P])
        ones = sb("ones", [P, P])
        eps = sb("eps", [P, 1])
        ones_r = sb("ones_r", [P, P], F32R)
        rows = sb("rows", [P, 2, NB, D], F32R)
        stateT = sb("stateT", [P, DB, N])
        fold = sb("fold", [P, 2, DB, NG, D], F32R)
        own = sb("own", [P, 2, DB, NG, D], F32R)
        o_w = sb("o_w", [P, 2, 2, DB, D], F32R)
        a8 = sb("a8", [P, NC, NB, CW], U8)
        ring = sb("ring", [P, RING, 2, CW], F32R)
        stage = sb("stage", [P, STAGES, 2, CW], I32)
        degree = sb("degree", [P, N], U16)
        st_c = sb("st_c", [P, 2, DB, CW], F32R)
        u_c = sb("u_c", [P, 2, DB, CW], F32R)
        rs_c = sb("rs_c", [P, 2, DB, CW], F32R)
        work = sb("work", [P, 8, CW])
        gates = work[:, 0:6, :].rearrange("p (g e) w -> p g e w", g=NG)
        tmp = work[:, 6:8, :]
        x_raw = work[:, :, :].rearrange("p a w -> p (a w)").rearrange("p (b d) -> p b d", d=D)
        bias = sb("bias", [P, NG + 1, DB])
        deg_w = sb("deg_w", [P, NG, DB])
        o2_bb = sb("o2_bb", [P, D])
        deg_sum = sb("deg_sum", [P, NB // 2 * CW // 4], U32)
        deg_part = sb("deg_part", [P, CW], F32R)
        stats = sb("stats", [P, NB, 6])
        mv = sb("mv", [P, NB, 2])
        std = sb("std", [P, NB])
        rstd = sb("rstd", [P, NB])
        shift = sb("shift", [P, NB])
        above = sb("above", [P, NC * NP])
        differ = sb("differ", [P, 2 * NC])
        odd = sb("odd", [P, 3])

        late = a8[:, 2:4, :, :].rearrange("p c b w -> p (c b w)").bitcast(F32)
        NR = DB * NG * D
        early = stateT[:, :, :].rearrange("p d n -> p (d n)")
        gate_raw = [g.rearrange("p (b k) -> p b k", b=DB) for g in (late[:, 0:NR], late[:, NR:2 * NR], early[:, 0:NR])]
        o_raw = late[:, 2 * NR:2 * NR + 2 * DB * D].rearrange("p (n b k) -> p n b k", n=2, b=DB)
        gate_T = [g.rearrange("p (m d) -> p m d", d=D) for g in (early[:, NR:NR + 2 * DB * D], degree[:, :].bitcast(F32))]
        lin_raw = early[:, NR + 2 * DB * D:NR + 4 * DB * D].rearrange("p (n b k) -> p n b k", n=2, b=DB)

        lin_bb = a8[:, 0, :, :].rearrange("p b w -> p (b w)").bitcast(F32)[:, 0:2 * D].rearrange("p (n d) -> p n d", n=2)
        deg_scratch = a8[:, 0, :, :].rearrange("p b w -> p (b w)").bitcast(F32)[:, 2 * D:4 * D]

        staged = [stage[:, n] for n in range(STAGES)]
        staged.append(a8[:, 0, NB // 2:, :].bitcast(I32).rearrange("p b w -> p (b w)").rearrange("p (j w) -> p j w", j=2))
        for h in range(2):
            staged.append(a8[:, 1, h * NB // 2:(h + 1) * NB // 2, :].bitcast(I32)
                          .rearrange("p b w -> p (b w)").rearrange("p (j w) -> p j w", j=2))
        staged.append(deg_sum[:, :].bitcast(I32).rearrange("p (j w) -> p j w", j=2))
        IN_CHUNK_0, IN_CHUNK_1, IN_SUMS = STAGES, STAGES + 2, STAGES + 3

        def slot_of(q):
            late_q = q - len(staged)
            return (q, 1) if late_q < 0 else (late_q % STAGES, late_q // STAGES + 2)

        PACK = 8
        NPK = NB // PACK
        flat_stage = stage[:, :, :, :].rearrange("p s a w -> p (s a w)")
        pack_rows = flat_stage[:, 0:NPK * N // 4].bitcast(U32).rearrange("p (g w) -> p g w", g=NPK)
        pack_cols = flat_stage[:, NPK * N // 4:2 * NPK * N // 4].bitcast(U32).rearrange("p (b g w) -> p b g w", b=NB, g=NPK)
        rows_u8 = flat_stage[:, 0:NPK * N // 4].bitcast(U8).rearrange("p (g c w) -> p g c w", g=NPK, c=NC)
        cols_u8 = flat_stage[:, NPK * N // 4:2 * NPK * N // 4].bitcast(U8).rearrange("p (b g w) -> p b g w", b=NB, g=NPK)
        scratch = deg_sum[:, 0:CW // 4].bitcast(U8)
        pack_f = flat_stage[:, 2 * NPK * N // 4:2 * NPK * N // 4 + 2 * CW].bitcast(F32).rearrange("p (n w) -> p n w", n=2)

        y = a8[:, 0:2, :, :].rearrange("p c b w -> p (c b w)").bitcast(F32).rearrange("p (b d) -> p b d", d=D)
        x_res = late.rearrange("p (b d) -> p b d", d=D)
        fin_c = [[rows[:, part, :, :].rearrange("p b d -> p (b d)")[:, c * DB * CW:(c + 1) * DB * CW]
                  .rearrange("p (k w) -> p k w", k=DB) for part in (HI, LO)] for c in range(NC)]
        hid_c = [[ring[:, 2 * n + part] for part in (HI, LO)] for n in range(2)]

        bank = [ctx.enter_context(nc.psum_tensor(f"bank{i}", [P, CW], F32)) for i in range(8)]
        u_bank = bank[0:4]
        g_bank = bank[4:7]
        t_bank = bank[7]

        def turn_bank(k, h):
            return t_bank if h == 0 else u_bank[2] if k == NC - 1 else u_bank[0]

        out_bank = [bank[2:4], bank[4:6], bank[6:8], bank[2:4]]

        stage_loaded = [sem(f"f_stage_loaded{i}") for i in range(len(staged))]
        x_loaded = sem("f_x_loaded")
        io_b_loaded = sem("f_io_b_loaded")
        b_loaded = sem("f_b_loaded")
        o2_b_loaded = sem("f_o2_b_loaded")
        w_loaded = [sem(f"f_w_loaded{g}") for g in range(NG)]
        lin_loaded = sem("f_lin_loaded")
        o_loaded = sem("f_o_loaded")
        byte_sum = sem("f_byte_sum")
        deg_summed = sem("f_deg_summed")
        deg_w_ready = sem("f_deg_w_ready")
        deg_part_ready = sem("f_deg_part_ready")
        degree_done = sem("f_degree_done")
        packed = sem("f_packed")
        pack_f_ready = sem("f_pack_f_ready")
        fin_hi = sem("f_fin_hi")
        fin_lo = sem("f_fin_lo")
        zeroed = sem("f_zeroed")
        const_ready = sem("f_const_ready")
        ones_ready = sem("f_ones_ready")
        x_hi = sem("f_x_hi")
        x_split = sem("f_x_split")
        x_turned = sem("f_x_turned")
        x_read = sem("f_x_read")
        prep_done = sem("f_prep_done")
        prep_hi = sem("f_prep_hi")
        prep_read = sem("f_prep_read")
        pair_stored = sem("f_pair_stored")
        pair_ready = sem("f_pair_ready")
        pair_used = sem("f_pair_used")
        check_done = sem("f_check_done")
        check_read = sem("f_check_read")
        degree_read = sem("f_degree_read")
        agg_done = sem("f_agg_done")
        u_hi = sem("f_u_hi")
        u_lo = sem("f_u_lo")
        u_used = sem("f_u_used")
        st_hi = sem("f_st_hi")
        st_lo = sem("f_st_lo")
        gate_done = sem("f_gate_done")
        gate_read = sem("f_gate_read")
        gate_act = sem("f_gate_act")
        rs_ready = sem("f_rs_ready")
        rs_hi = sem("f_rs_hi")
        rs_lo = sem("f_rs_lo")
        turn_done = sem("f_turn_done")
        row_hi = sem("f_row_hi")
        row_lo = sem("f_row_lo")
        state_new = sem("f_state_new")
        chain = sem("f_chain")
        odd_link = sem("f_odd_link")
        odd_ready = sem("f_odd_ready")
        odd_done = sem("f_odd_done")
        hid_done = sem("f_hid_done")
        hid_act = sem("f_hid_act")
        hid_hi = sem("f_hid_hi")
        hid_lo = sem("f_hid_lo")
        hid_lo_pool = sem("f_hid_lo_pool")
        fin_lo_pool = sem("f_fin_lo_pool")
        state_new_pool = sem("f_state_new_pool")
        pool_chain = sem("f_pool_chain")
        o_done = sem("f_o_done")
        o_read = sem("f_o_read")
        xr_loaded = sem("f_xr_loaded")
        residual_ready = sem("f_residual_ready")
        stats_ready = sem("f_stats_ready")
        aggr_ready = sem("f_aggr_ready")
        std_first = sem("f_std_first")
        shift_ready = sem("f_shift_ready")
        rstd_ready = sem("f_rstd_ready")
        y_dve = sem("f_y_dve")
        y_pool = sem("f_y_pool")
        y_act = sem("f_y_act")
        std_ready = sem("f_std_ready")
        y_stored = sem("f_y_stored")

        N_PREP = NG * 4 + 2
        PREP = [(k, 0) for k in (0, 1, "own")]
        for g in range(NG):
            PREP += [(k, g + 1) for k in (0, 1, "own")] if g + 1 < NG else []
            PREP += [("fold", g)]
        PREP += [("o", 0), ("o", 1)]
        ACT_AHEAD = {("fold", 1): [("x", 0), ("x", 1)], ("o", 1): [("pair", 0), ("pair", 1)]}
        DVE_AHEAD = {("own", 0): [("degree", 0)], ("own", 1): [("degree", 1)], ("fold", 1): [("degree", 2), ("x", 0)],
                     ("o", 1): [("x", 1), ("x", 2), ("x", 3)]}
        def prep_bank(n):
            return bank[(n + 8 - N_PREP % 8) % 8]

        out_v = out.rearrange("(b p) d -> p b d", p=P)
        x_v = x.rearrange("(b p) d -> p b d", p=P)
        adj_v = adj.rearrange("(j p) i -> p j i", p=P)
        BATCHES = [(0, NB - 2 * BC), (NB - 2 * BC, NB - BC), (NB - BC, NB)]
        BY_DVE = [NB - 6, NB - 4, NB - 2]
        BY_POOL = [2, 5, 9]
        TREE = [NB // 2 * CW // 4 >> n for n in range(4)]

        block = ctx.enter_context(nc.Block())

        @block.sync
        def _(sp):
            for g, w in enumerate((r_W, z_W, h_W)):
                sp.dma_start(gate_raw[g], w.rearrange("(b p) k -> p b k", p=P)).then_inc(w_loaded[g], 16)
                if g == 1:
                    for n, w in enumerate((in_W, out_W)):
                        sp.dma_start(lin_raw[:, n], w.rearrange("(b p) k -> p b k", p=P)).then_inc(lin_loaded, 16)
            sp.dma_start(x_raw, x_v).then_inc(x_loaded, 16)
            for n, w in enumerate((o1_W, o2_W)):
                sp.dma_start(o_raw[:, n], w.rearrange("(b p) k -> p b k", p=P)).then_inc(o_loaded, 16)
            for c in range(NC):
                for p in range(NP):
                    q = c * NP + p
                    slot, loads = slot_of(q)
                    if loads > 1:
                        before = slot if loads == 2 else q - STAGES
                        sp.wait_ge(pair_ready, before + 1)
                        sp.wait_ge(pair_stored, before + 1)
                    sp.dma_start(staged[slot], adj_v[:, 2 * p:2 * p + 2, c * CW:(c + 1) * CW]).then_inc(stage_loaded[slot], 16)
            sp.wait_ge(pair_ready, N_STEPS * S_PAIR)
            sp.dma_start(x_res, x_v).then_inc(xr_loaded, 16)
            starts = [c * BC for c in range(NC)] + [NB - BC // 2, NB]
            for a, b in zip(starts, starts[1:]):
                dve_blocks, pool_blocks = (sum(m < b for m in blocks) for blocks in (BY_DVE, BY_POOL))
                wait(sp, y_dve, dve_blocks)
                wait(sp, y_pool, pool_blocks)
                sp.wait_ge(y_act, b - dve_blocks - pool_blocks)
                sp.dma_start(out_v[:, a:b, :], y[:, a:b, :]).then_inc(y_stored, 16)
            sp.wait_ge(y_stored, 16 * (len(starts) - 1))

        @block.gpsimd
        def _(pool):
            nc.gpsimd.memset(ident[:, :], 0.0).then_inc(zeroed, 1)
            nc.gpsimd.memset(ones[:, :], 1.0).then_inc(const_ready, 1)
            nc.gpsimd.memset(eps[:, :], EPS).then_inc(const_ready, 1)
            pool.wait_ge(zeroed, 1)
            nc.gpsimd.affine_select(out=ident[:, :], in_=ident[:, :], compare_op=ALU.not_equal, fill=1.0,
                                    base=0, pattern=[[-1, P]], channel_multiplier=1).then_inc(const_ready, 1)

            def add(out_, a, b, s):
                nc.gpsimd.tensor_tensor(out_, a, b, ALU.add).then_inc(s, 1)

            words = a8[:, :, :, :].rearrange("p c b w -> p c (b w)").bitcast(U32)
            n = 0
            for c in range(NC):
                pool.wait_ge(pair_stored, (c + 1) * NP)
                pool.wait_ge(pair_ready, IN_SUMS + 1)
                wait(pool, deg_part_ready, c)
                for level, w in enumerate(TREE):
                    src = words[:, c, :] if level == 0 else deg_sum[:, :]
                    wait(pool, byte_sum, n)
                    add(deg_sum[:, 0:w], src[:, 0:w], src[:, w:2 * w], deg_summed if level == len(TREE) - 1 else byte_sum)
                    n += level < len(TREE) - 1
            pool.wait_ge(pair_ready, S_PAIR)
            pool.wait_ge(pair_stored, S_PAIR)
            n = 0
            for g in range(NPK):
                def row_block(k):
                    return a8[:, :, PACK * g + k, :].bitcast(U32)

                def col_block(k):
                    m = PACK * g + k
                    return a8[:, m // BC, :, m % BC * P:(m % BC + 1) * P].bitcast(U32)

                for acc, block_of in ((pack_rows[:, g, :].rearrange("p (c w) -> p c w", c=NC), row_block),
                                      (pack_cols[:, :, g, :], col_block)):
                    for k in reversed(range(PACK - 1)):
                        twice = block_of(PACK - 1) if k == PACK - 2 else acc
                        wait(pool, packed, n)
                        add(acc, twice, twice, packed)
                        pool.wait_ge(packed, n + 1)
                        add(acc, acc, block_of(k), packed)
                        n += 2
            pool.wait_ge(o2_b_loaded, 16)
            pool.wait_ge(xr_loaded, 16)
            for c in range(NC):
                xr = x_res[:, c * BC:(c + 1) * BC, :]
                nc.gpsimd.tensor_tensor(xr, xr, o2_bb[:, :].unsqueeze(1).broadcast_to([P, BC, D]), ALU.add)\
                    .then_inc(residual_ready, 1)

            def low(out_, in_, hi_, s):
                nc.gpsimd.tensor_tensor(out_, in_, hi_.bitcast(F32), ALU.subtract).then_inc(s, 1)

            def split_hidden(c):
                pool.wait_ge(hid_hi, (c + 1) * DB)
                low(hid_c[c % 2][LO][:, 1, :], stateT[:, 1, c * CW:(c + 1) * CW], hid_c[c % 2][HI][:, 1, :], hid_lo_pool)

            split_hidden(1)
            c, e = NC - 1, 1
            old = stateT[:, e, c * CW:(c + 1) * CW]
            pool.wait_ge(gate_act, N_STEPS * S_GATE)
            nc.gpsimd.tensor_tensor(tmp[:, e, :], gates[:, H, e, :], old, ALU.subtract).then_inc(pool_chain, 1)
            pool.wait_ge(pool_chain, 1)
            nc.gpsimd.tensor_tensor(tmp[:, e, :], tmp[:, e, :], gates[:, Z, e, :], ALU.mult).then_inc(pool_chain, 1)
            pool.wait_ge(pool_chain, 2)
            nc.gpsimd.tensor_tensor(old, old, tmp[:, e, :], ALU.add).then_inc(state_new_pool, 1)

            pool.wait_ge(fin_hi, NC * DB)
            low(fin_c[c][LO][:, e, :], old, fin_c[c][HI][:, e, :], fin_lo_pool)
            split_hidden(2)
            split_hidden(3)
            for m in BY_POOL:
                pool.wait_ge(shift_ready, 1 + (m >= BATCHES[0][1]))
                nc.gpsimd.tensor_scalar(y[:, m, :], y[:, m, :], mv[:, m, 0:1], rstd[:, m:m + 1],
                                        ALU.subtract, ALU.mult).then_inc(y_pool, 1)

        @block.tensor
        def _(pe):
            def three(out_, wh, wl, vh, vl, first, last):
                nc.tensor.matmul(out_, wh, vh, start=first, stop=False)
                nc.tensor.matmul(out_, wh, vl, start=False, stop=False)
                return nc.tensor.matmul(out_, wl, vh, start=False, stop=last)

            def check_turn(n):
                pe.wait_ge(pack_f_ready, n + 1)
                wait(pe, check_read, n)
                for b in range(BC):
                    last = nc.tensor.transpose(t_bank[:, b * P:(b + 1) * P], pack_f[:, n % 2, b * P:(b + 1) * P], ident[:, :])
                last.then_inc(check_done, 1)

            def degrees(c):
                pe.wait_ge(deg_part_ready, c + 1)
                if c == NC - 1:
                    pe.wait_ge(row_lo, sum(k[0] < c for k in T_AT))
                nc.tensor.matmul(t_bank[:, :], ones_r[:, :], deg_part[:, :], start=True, stop=True).then_inc(degree_done, 1)

            def turn(t, k, h, first=False):
                wait(pe, state_new, t * S_TWO + (k + 1) * TWO)
                wait(pe, row_lo, t * S_TWO + 2 * k + h - 1)
                if first:
                    pe.wait_ge(degree_read, NC if k == 2 else NC - 1)
                for j in range(2):
                    for d in range(DB):
                        b = k * BC + 2 * h + j
                        last = nc.tensor.transpose(turn_bank(k, h)[:, (j * DB + d) * P:(j * DB + d + 1) * P],
                                                   stateT[:, d, b * P:(b + 1) * P], ident[:, :])
                last.then_inc(turn_done, 1)

            def aggregate(t, c, first=False):
                wait(pe, u_lo, t * S_TWO + (c - 1) * TWO)
                if first:
                    pe.wait_ge(x_read, min(NC * DB, (c + 1) * TWO))
                elif c == 0:
                    pe.wait_ge(row_lo, (t - 1) * S_TWO + 2 * (NC - 1))
                for p in range(NP):
                    pe.wait_ge(pair_ready, t * S_PAIR + c * NP + p + 1)
                    if c == 0 and not first:
                        if p == 4:
                            turn(t - 1, NC - 1, 0)
                        if p == 5:
                            turn(t - 1, NC - 1, 1)
                        pe.wait_ge(row_lo, (t - 1) * S_TWO + p + 1)
                    if c == 0 and first:
                        pe.wait_ge(x_split, p // 2 + 1)
                    for jj in range(2):
                        j = 2 * p + jj
                        for d in range(DB):
                            for part in (HI, LO):
                                last = nc.tensor.matmul(u_bank[2 * (c % 2) + d][:, :], rows[:, part, j, d * P:(d + 1) * P],
                                                        ring[:, p % RING, jj, :], start=(j == 0 and part == HI),
                                                        stop=(j == NB - 1 and part == LO))
                            if j == NB - 1 and d == 0:
                                last.then_inc(agg_done, 1)
                    last.then_inc(pair_used, 1)

            def gate_chunk(t, c, first=False, last_step=False):
                if first:
                    if c == 0:
                        pe.wait_ge(x_read, NC * DB)
                    degrees(c)
                pe.wait_ge(st_lo, t * S_TWO + (c + 1) * TWO)
                for s in range(2 * DB):
                    g, e = s // DB, s % DB
                    wait(pe, gate_read, t * S_GATE + c * GATE + s - 2)
                    own_part(g_bank[s % 3], g, e, st_c)
                    if (c, s) in T_AT and not last_step:
                        turn(t, *T_AT[c, s], first)
                    if last_step and c < NPK:
                        check_turn(c * NC + s)
                    if last_step and (c, s) == (NPK, 1):
                        count_odd()
                    if s == 0:
                        pe.wait_ge(u_lo, t * S_TWO + (c + 1) * TWO)
                    fold_part(g_bank[s % 3], g, e, False).then_inc(gate_done, 1)
                for e in range(DB):
                    s = 2 * DB + e
                    wait(pe, gate_read, t * S_GATE + c * GATE + s - 2)
                    last = fold_part(g_bank[s % 3], H, e, True)
                last.then_inc(u_used, 1)
                if last_step and c == NC - 1:
                    hidden(1)
                pe.wait_ge(rs_lo, t * S_TWO + (c + 1) * TWO)
                for e in range(DB):
                    own_part(g_bank[(2 * DB + e) % 3], H, e, rs_c, True).then_inc(gate_done, 1)

            def own_part(b, g, e, v, last=False):
                for k in range(DB):
                    m = three(b[:, :], own[:, HI, k, g, e * P:(e + 1) * P], own[:, LO, k, g, e * P:(e + 1) * P],
                              v[:, HI, k, :], v[:, LO, k, :], k == 0 and not last, k == DB - 1 and last)
                return m

            def fold_part(b, g, e, first):
                for k in range(DB):
                    m = three(b[:, :], fold[:, HI, k, g, e * P:(e + 1) * P], fold[:, LO, k, g, e * P:(e + 1) * P],
                              u_c[:, HI, k, :], u_c[:, LO, k, :], k == 0 and first, k == DB - 1 and not first)
                return m

            def step(t, first=False):
                aggregate(t, 0, first)
                aggregate(t, 1, first)
                for c in range(NC):
                    gate_chunk(t, c, first)
                    if c + 2 < NC:
                        aggregate(t, c + 2, first)

            def turn_x():
                pe.wait_ge(x_loaded, 16)
                for c in range(NC):
                    for d in range(DB):
                        m = c * DB + d
                        pe.wait_ge(prep_read, N_PREP + m - 7)
                        for b in range(BC):
                            last = nc.tensor.transpose(bank[m][:, b * P:(b + 1) * P],
                                                       x_raw[:, c * BC + b, d * P:(d + 1) * P], ident[:, :])
                        last.then_inc(x_turned, 1)

            def prepare():
                for n, (kind, g) in enumerate(PREP):
                    b_ = prep_bank(n)
                    wait(pe, prep_read, n - 7)
                    if kind == "fold":
                        if g == 0:
                            pe.wait_ge(lin_loaded, 32)
                        pe.wait_ge(prep_read, PREP.index((1, g)) + 1)
                        for k in range(DB):
                            for m in range(2 * DB):
                                last = nc.tensor.matmul(b_[:, k * D:(k + 1) * D], lin_raw[:, m // DB, m % DB, k * P:(k + 1) * P],
                                                        gate_T[g % 2][:, m, :], start=(m == 0), stop=(m == 2 * DB - 1))
                    else:
                        if kind == 0:
                            pe.wait_ge(w_loaded[g], 16)
                        if (kind, g) == ("o", 0):
                            pe.wait_ge(o_loaded, 32)
                        raw = o_raw[:, g] if kind == "o" else gate_raw[g]
                        first_block = {0: 0, 1: DB, "own": 2 * DB, "o": 0}[kind]
                        for k in range(DB):
                            for b in range(DB):
                                kk = first_block + k
                                last = nc.tensor.transpose(b_[:, (k * DB + b) * P:(k * DB + b + 1) * P],
                                                           raw[:, b, kk * P:(kk + 1) * P], ident[:, :])
                    last.then_inc(prep_done, 1)

            def count_odd():
                pe.wait_ge(odd_ready, 1)
                nc.tensor.matmul(t_bank[0:1, 0:1], odd[:, 2:3], ones[:, 0:1], start=True, stop=True).then_inc(odd_done, 1)

            def hidden(c):
                v = fin_c[c]
                if c < NC - 1:
                    pe.wait_ge(fin_lo, (c + 1) * DB)
                else:
                    pe.wait_ge(fin_lo, c * DB + 1)
                    pe.wait_ge(fin_lo_pool, 1)
                for e in range(DB):
                    wait(pe, hid_act, (c - 1) * DB + e + 1)
                    for k in range(DB):
                        last = three(u_bank[e][:, :], o_w[:, HI, 0, k, e * P:(e + 1) * P], o_w[:, LO, 0, k, e * P:(e + 1) * P],
                                     v[HI][:, k, :], v[LO][:, k, :], k == 0, k == DB - 1)
                    last.then_inc(hid_done, 1)

            def output(c):
                pe.wait_ge(hid_lo, DB + c)
                wait(pe, hid_lo_pool, c)
                if c == 1:
                    pe.wait_ge(gate_read, N_STEPS * S_GATE)
                if c == NC - 1:
                    pe.wait_ge(o_read, BC // 2)
                v = hid_c[c % 2]
                for b in range(BC):
                    for k in range(DB):
                        last = three(out_bank[c][b // 2][:, b % 2 * D:(b % 2 + 1) * D],
                                     v[HI][:, k, b * P:(b + 1) * P], v[LO][:, k, b * P:(b + 1) * P],
                                     o_w[:, HI, 1, k, :], o_w[:, LO, 1, k, :], k == 0, k == DB - 1)
                    if b % 2 == 1:
                        last.then_inc(o_done, 1)

            pe.wait_ge(const_ready, 3)
            pe.wait_ge(ones_ready, 1)
            for _ in range(WARM_UP):
                nc.tensor.matmul(bank[1][:, 0:P], ident[:, :], ones[:, :], start=True, stop=True)
            prepare()
            turn_x()
            step(0, first=True)
            with pe.Fori(1, LAST) as t:
                step(t)
            aggregate(LAST, 0)
            aggregate(LAST, 1)
            for c in range(NC):
                gate_chunk(LAST, c, last_step=True)
                if c + 2 < NC:
                    aggregate(LAST, c + 2)
                if c == NC - 2:
                    hidden(0)
            output(0)
            hidden(2)
            output(1)
            hidden(3)
            output(2)
            output(3)

        @block.scalar
        def _(act):
            def high(out_, in_, s):
                nc.scalar.activation(out_, in_, ACT.Copy).then_inc(s, 1)

            def expand_staged(c, p):
                q = c * NP + p
                wait(act, pair_used, q + 1 - RING)
                slot, loads = slot_of(q)
                act.wait_ge(stage_loaded[slot], 16 * loads)
                high(ring[:, p % RING], staged[slot], pair_ready)

            def split_u(t, c, d):
                if d == 0:
                    act.wait_ge(agg_done, t * NC + c + 1)
                else:
                    act.wait_ge(pair_used, t * S_PAIR + (c + 1) * NP)
                wait(act, u_used, t * NC + c)
                high(u_c[:, HI, d, :], u_bank[2 * (c % 2) + d][:, :], u_hi)

            def split_state(t, c, e):
                if not (isinstance(t, int) and t == 0):
                    act.wait_ge(state_new, (t - 1) * S_TWO + c * TWO + e + 1)
                wait(act, gate_done, t * S_GATE + (c - 1) * GATE + 2 * DB)
                high(st_c[:, HI, e, :], stateT[:, e, c * CW:(c + 1) * CW], st_hi)

            def row_high(t, k, h):
                act.wait_ge(turn_done, t * S_TWO + 2 * k + h + 1)
                b = k * BC + 2 * h
                high(rows[:, HI, b:b + 2, :].rearrange("p b d -> p (b d)"), turn_bank(k, h)[:, :], row_hi)

            def gate(t, c, s):
                act.wait_ge(gate_read, t * S_GATE + c * GATE + s + 1)
                g, e = s // DB, s % DB
                nc.scalar.activation(gates[:, g, e, :], gates[:, g, e, :], ACT.Tanh if g == H else ACT.Sigmoid,
                                     bias=bias[:, g, e:e + 1]).then_inc(gate_act, 1)

            def rs_high(t, c, e):
                wait(act, gate_done, t * S_GATE + c * GATE)
                act.wait_ge(rs_ready, t * S_TWO + c * TWO + e + 1)
                high(rs_c[:, HI, e, :], tmp[:, e, :], rs_hi)

            def gate_chunk(t, c, first, last):
                if first and c < NC - 1:
                    degree_part(c)
                for s in range(GATE):
                    if (c, s) in T_AT and not last:
                        row_high(t, *T_AT[c, s])
                    gate(t, c, s)
                    if s < DB:
                        rs_high(t, c, s)
                    if last and (c, s) in FINAL_AT:
                        final_split(FINAL_AT[c, s])
                    if s < DB:
                        continue
                    if first and c + 2 < NC and s < 2 * DB:
                        expand_staged(c + 2, 2 * (s - DB))
                        expand_staged(c + 2, 2 * (s - DB) + 1)
                    if c == NC - 2 and s == 2 * DB - 1:
                        if first:
                            degree_part(NC - 1)
                        for e in range(DB):
                            split_state(t, NC - 1, e)
                        for d in range(DB):
                            split_u(t, NC - 1, d)
                    if last and (c, s) == (NC - 2, GATE - 1):
                        hidden(0)
                    if last and (c, s) == (NC - 1, 2 * DB - 1):
                        hidden(1)

            def degree_part(c):
                act.wait_ge(deg_summed, c + 1)
                wait(act, degree_done, c)
                high(deg_part[:, :], deg_sum[:, 0:TREE[-1]].bitcast(U8), deg_part_ready)

            def final_split(c):
                for e in range(DB):
                    if (c, e) == (NC - 1, 1):
                        act.wait_ge(state_new_pool, 1)
                    else:
                        act.wait_ge(state_new, LAST * S_TWO + c * TWO + e + 1)
                    high(fin_c[c][HI][:, e, :], stateT[:, e, c * CW:(c + 1) * CW], fin_hi)

            def hidden(c):
                hid = stateT[:, :, c * CW:(c + 1) * CW]
                for e in range(DB):
                    act.wait_ge(hid_done, c * DB + e + 1)
                    nc.scalar.activation(hid[:, e, :], u_bank[e][:, :], ACT.Tanh, bias=bias[:, NG, e:e + 1]).then_inc(hid_act, 1)
                for e in range(DB):
                    act.wait_ge(hid_act, c * DB + e + 1)
                    wait(act, o_done, (c - 1) * (BC // 2))
                    high(hid_c[c % 2][HI][:, e, :], hid[:, e, :], hid_hi)

            def aggregate(t, c, first):
                for n in range(2 * DB):
                    if first:
                        expand_staged(c, LEAD + n)
                    if n < DB:
                        split_u(t, c - 1, n)
                    else:
                        split_state(t, c - 1, n - DB)

            def step(t, first=False, last=False):
                if first:
                    for m in range(DB):
                        turned_x(m)
                    for m in range(2, NC):
                        x_high(m)
                    for p in range(DB, NP):
                        expand_staged(0, p)
                        turned_x(p)
                    act.wait_ge(x_read, NC * DB)
                    for p in range(LEAD):
                        expand_staged(1, p)
                else:
                    for h in range(2):
                        row_high(t - 1, NC - 1, h)
                aggregate(t, 1, first)
                for c in range(NC):
                    gate_chunk(t, c, first, last)
                    if c + 2 < NC:
                        aggregate(t, c + 2, first)

            def prepare():
                for n, (kind, g) in enumerate(PREP):
                    if kind in ("own", "fold", "o"):
                        dst = o_w[:, HI, g] if kind == "o" else (own if kind == "own" else fold)[:, HI, :, g, :]
                        act.wait_ge(prep_done, n + 1)
                        high(dst, prep_bank(n)[:, :].rearrange("p (k d) -> p k d", d=D), prep_hi)
                    for what, m in ACT_AHEAD.get((kind, g), ()):
                        if what == "x":
                            x_high(m)
                        else:
                            expand_staged(0, m)

            def x_high(m):
                act.wait_ge(x_loaded, 16)
                high(rows[:, HI, m * BC:(m + 1) * BC, :], x_raw[:, m * BC:(m + 1) * BC, :], x_hi)

            def turned_x(m):
                act.wait_ge(x_turned, m + 1)
                nc.scalar.activation(stateT[:, m % DB, m // DB * CW:(m // DB + 1) * CW], bank[m][:, :], ACT.Copy)\
                  .then_inc(x_read, 1)

            for n, b in enumerate((in_b, out_b)):
                act.dma_start(lin_bb[:, n], b.partition_broadcast(P)).then_inc(io_b_loaded, 16)
            for n, b in ((R, r_b), (Z, z_b), (H, h_b), (NG, o1_b)):
                act.dma_start(bias[:, n], b.rearrange("(b p) -> p b", p=P), allow_slow_non_contiguous=True)\
                   .then_inc(b_loaded, 16)
            act.dma_start(o2_bb[:, :], o2_b.partition_broadcast(P)).then_inc(o2_b_loaded, 16)
            prepare()
            act.wait_ge(prep_read, N_PREP)
            act.wait_ge(b_loaded, 16 * (NG + 1))
            step(0, first=True)
            with act.Fori(1, LAST) as t:
                step(t)
            step(LAST, last=True)

            final_split(3)
            hidden(2)
            hidden(3)
            nc.scalar.activation(std[:, 0:1], ones[:, 0:1], ACT.Sqrt).then_inc(std_first, 1)
            act.wait_ge(std_first, 1)
            for n, (a, b) in enumerate(BATCHES):
                act.wait_ge(aggr_ready, b)
                nc.scalar.activation(std[:, a:b], mv[:, a:b, 1], ACT.Sqrt, bias=eps[:, 0:1]).then_inc(std_ready, 1)
                act.wait_ge(shift_ready, n + 1)
                for m in range(a, b):
                    if m not in BY_DVE + BY_POOL:
                        nc.scalar.activation(y[:, m, :], y[:, m, :], ACT.Identity, scale=rstd[:, m:m + 1],
                                             bias=shift[:, m:m + 1]).then_inc(y_act, 1)

        @block.vector
        def _(dve):
            def low(out_, in_, hi_, s):
                nc.vector.tensor_tensor(out_, in_, hi_.bitcast(F32), ALU.subtract).then_inc(s, 1)

            def expand(t, c, p):
                wait(dve, pair_used, t * S_PAIR + c * NP + p + 1 - RING)
                nc.vector.tensor_copy(ring[:, p % RING], a8[:, c, 2 * p:2 * p + 2, :]).then_inc(pair_ready, 1)

            def store_pair(c, p):
                q = c * NP + p
                slot, loads = slot_of(q)
                dve.wait_ge(stage_loaded[slot], 16 * loads)
                if q == 0:
                    dve.wait_ge(deg_w_ready, NG * DB)
                if q in (NP // 2, NP):
                    dve.wait_ge(pair_ready, (IN_CHUNK_0 if q < NP else IN_CHUNK_1) + 1)
                    dve.wait_ge(pair_stored, (IN_CHUNK_0 if q < NP else IN_CHUNK_1) + 1)
                nc.vector.tensor_scalar(a8[:, c, 2 * p:2 * p + 2, :], staged[slot].bitcast(U32), 1.0, 0.0,
                                        ALU.mult, ALU.max, accum_out=above[:, q:q + 1]).then_inc(pair_stored, 1)

            def check_expand(n):
                wait(dve, check_done, n - 1)
                nc.vector.tensor_copy(pack_f[:, n % 2, :], rows_u8[:, n // NC, n % NC, :]).then_inc(pack_f_ready, 1)

            def check(n):
                dve.wait_ge(check_done, n + 1)
                wait(dve, check_read, n)
                nc.vector.scalar_tensor_tensor(
                    out=scratch.rearrange("p (b q) -> p b q", b=BC), in0=t_bank[:, :].rearrange("p (b q) -> p b q", b=BC),
                    scalar=1.0, in1=cols_u8[:, n % NC * BC:(n % NC + 1) * BC, n // NC, :],
                    op0=ALU.mult, op1=ALU.not_equal, accum_out=differ[:, n:n + 1]).then_inc(check_read, 1)

            def pair(t, c, p, first):
                if first:
                    store_pair(c, p)
                else:
                    expand(t, c, p)

            def split_u(t, c, d):
                dve.wait_ge(u_hi, t * S_TWO + c * TWO + d + 1)
                low(u_c[:, LO, d, :], u_bank[2 * (c % 2) + d][:, :], u_c[:, HI, d, :], u_lo)

            def split_state(t, c, e):
                dve.wait_ge(st_hi, t * S_TWO + c * TWO + e + 1)
                low(st_c[:, LO, e, :], stateT[:, e, c * CW:(c + 1) * CW], st_c[:, HI, e, :], st_lo)

            def row_low(t, k, h):
                dve.wait_ge(row_hi, t * S_TWO + 2 * k + h + 1)
                b = k * BC + 2 * h
                low(rows[:, LO, b:b + 2, :].rearrange("p b d -> p (b d)"), turn_bank(k, h)[:, :],
                    rows[:, HI, b:b + 2, :].rearrange("p b d -> p (b d)"), row_lo)

            def gate(t, c, s):
                g, e = s // DB, s % DB
                dve.wait_ge(gate_done, t * S_GATE + c * GATE + s + 1)
                nc.vector.scalar_tensor_tensor(out=gates[:, g, e, :], in0=degree[:, c * CW:(c + 1) * CW],
                                               scalar=deg_w[:, g, e:e + 1], in1=g_bank[s % 3][:, :],
                                               op0=ALU.mult, op1=ALU.add).then_inc(gate_read, 1)

            def rs(t, c, e):
                dve.wait_ge(gate_act, t * S_GATE + c * GATE + e + 1)
                nc.vector.tensor_tensor(tmp[:, e, :], gates[:, R, e, :], stateT[:, e, c * CW:(c + 1) * CW],
                                        ALU.mult).then_inc(rs_ready, 1)

            def rs_low(t, c, e):
                dve.wait_ge(rs_hi, t * S_TWO + c * TWO + e + 1)
                low(rs_c[:, LO, e, :], tmp[:, e, :], rs_c[:, HI, e, :], rs_lo)

            def update(t, c):
                old = [stateT[:, e, c * CW:(c + 1) * CW] for e in range(DB)]
                n = 2 * (t * S_TWO + c * TWO)
                for e in range(DB):
                    dve.wait_ge(gate_act, t * S_GATE + c * GATE + H * DB + e + 1)
                    nc.vector.tensor_tensor(tmp[:, e, :], gates[:, H, e, :], old[e], ALU.subtract).then_inc(chain, 1)
                for e in range(DB):
                    dve.wait_ge(chain, n + e + 1)
                    nc.vector.tensor_tensor(tmp[:, e, :], tmp[:, e, :], gates[:, Z, e, :], ALU.mult).then_inc(chain, 1)
                for e in range(DB):
                    dve.wait_ge(chain, n + DB + e + 1)
                    nc.vector.tensor_tensor(old[e], old[e], tmp[:, e, :], ALU.add).then_inc(state_new, 1)

            def gate_chunk(t, c, first, last):
                if c + 2 < NC:
                    ahead = (t, c + 2, first)
                elif c == NC - 2 and not last:
                    ahead = (t + 1, 0, False)
                else:
                    ahead = None

                def next_pair(p):
                    if ahead:
                        pair(ahead[0], ahead[1], p, ahead[2])

                def turned(s):
                    if (c, s) in T_AT and not last:
                        row_low(t, *T_AT[c, s])

                def final(s):
                    if last and (c, s) in FINAL_AT:
                        final_split(FINAL_AT[c, s])
                    if last and (c, s) == (NC - 1, 0):
                        split_hidden(0)

                def last_check(s):
                    if last and c < NPK:
                        n = c * NC + s
                        check(n)
                        if n + 2 < NPK * NC:
                            check_expand(n + 2)

                if first:
                    dve.wait_ge(degree_done, c + 1)
                    nc.vector.tensor_copy(degree[:, c * CW:(c + 1) * CW], t_bank[:, :]).then_inc(degree_read, 1)
                    dve.wait_ge(degree_read, c + 1)
                if c == NC - 1:
                    update(t, c - 1)
                turned(0)
                last_check(0)
                gate(t, c, 0)
                final(0)
                next_pair(0)
                rs(t, c, 0)
                turned(1)
                last_check(1)
                gate(t, c, 1)
                rs_low(t, c, 0)
                rs(t, c, 1)
                final(1)
                next_pair(1)
                if last and c == NPK:
                    odd_flag()
                last_check(2)
                gate(t, c, 2)
                turned(2)
                rs_low(t, c, 1)
                final(2)
                next_pair(2)
                turned(3)
                last_check(3)
                gate(t, c, 3)
                next_pair(3)
                if c == NC - 2:
                    for e in range(DB):
                        split_state(t, NC - 1, e)
                    for d in range(DB):
                        split_u(t, NC - 1, d)
                gate(t, c, 4)
                gate(t, c, 5)

            def aggregate(t, c, first):
                if c >= 2:
                    update(t, c - 2)
                for n in range(2 * DB):
                    pair(t, c, LEAD + n, first)
                    if n < DB:
                        split_u(t, c - 1, n)
                    else:
                        split_state(t, c - 1, n - DB)

            def step(t, first=False, last=False):
                if first:
                    for p in range(NP):
                        store_pair(0, p)
                    for p in range(LEAD):
                        store_pair(1, p)
                else:
                    update(t - 1, NC - 1)
                    expand(t, 0, 4)
                    expand(t, 0, 5)
                    row_low(t - 1, NC - 1, 0)
                    expand(t, 0, 6)
                    row_low(t - 1, NC - 1, 1)
                    expand(t, 0, 7)
                    for p in range(LEAD):
                        expand(t, 1, p)
                aggregate(t, 1, first)
                if last:
                    dve.wait_ge(packed, 2 * 2 * NPK * (PACK - 1))
                    check_expand(0)
                    check_expand(1)
                for c in range(NC):
                    gate_chunk(t, c, first, last)
                    if last and c == NPK - 1:
                        odd_count()
                    if c + 2 < NC:
                        aggregate(t, c + 2, first)

            def prepare():
                hi = 0
                for n, (kind, g) in enumerate(PREP):
                    if kind in ("own", "fold", "o"):
                        dst = o_w[:, :, g] if kind == "o" else (own if kind == "own" else fold)[:, :, :, g, :]
                        hi += 1
                        dve.wait_ge(prep_hi, hi)
                        low(dst[:, LO], prep_bank(n)[:, :].rearrange("p (k d) -> p k d", d=D), dst[:, HI], prep_read)
                    else:
                        dve.wait_ge(prep_done, n + 1)
                        nc.vector.tensor_copy(gate_T[g % 2][:, kind * DB:(kind + 1) * DB, :].rearrange("p k d -> p (k d)"),
                                              prep_bank(n)[:, :]).then_inc(prep_read, 1)
                    for what, m in DVE_AHEAD.get((kind, g), ()):
                        if what == "x":
                            dve.wait_ge(x_hi, m + 1)
                            low(rows[:, LO, m * BC:(m + 1) * BC, :], x_raw[:, m * BC:(m + 1) * BC, :],
                                rows[:, HI, m * BC:(m + 1) * BC, :], x_split)
                        else:
                            degree_weight(m)

            def degree_weight(g):
                if g == 0:
                    dve.wait_ge(io_b_loaded, 32)
                dve.wait_ge(w_loaded[g], 16)
                for e in range(DB):
                    wait(dve, deg_w_ready, g * DB + e)
                    nc.vector.scalar_tensor_tensor(
                        out=deg_scratch, in0=gate_raw[g][:, e, 0:2 * D], scalar=1.0, in1=lin_bb.rearrange("p n d -> p (n d)"),
                        op0=ALU.mult, op1=ALU.mult, accum_out=deg_w[:, g, e:e + 1]).then_inc(deg_w_ready, 1)

            def final_split(c):
                for e in range(1 if c == NC - 1 else DB):
                    dve.wait_ge(fin_hi, c * DB + e + 1)
                    low(fin_c[c][LO][:, e, :], stateT[:, e, c * CW:(c + 1) * CW], fin_c[c][HI][:, e, :], fin_lo)

            def split_hidden(c):
                for e in range(DB if c == 0 else 1):
                    dve.wait_ge(hid_hi, c * DB + e + 1)
                    low(hid_c[c % 2][LO][:, e, :], stateT[:, e, c * CW:(c + 1) * CW], hid_c[c % 2][HI][:, e, :], hid_lo)

            def odd_count():
                dve.wait_ge(check_read, NPK * NC)
                nc.vector.tensor_scalar(above[:, :], above[:, :], 1.0, 0.0, ALU.is_gt, ALU.add,
                                        accum_out=odd[:, 0:1]).then_inc(odd_link, 1)
                nc.vector.tensor_scalar(differ[:, :], differ[:, :], 1.0, 0.0, ALU.mult, ALU.add,
                                        accum_out=odd[:, 1:2]).then_inc(odd_link, 1)
                dve.wait_ge(odd_link, 2)
                nc.vector.tensor_tensor(odd[:, 2:3], odd[:, 0:1], odd[:, 1:2], ALU.add).then_inc(odd_ready, 1)

            def odd_flag():
                dve.wait_ge(odd_done, 1)
                nc.vector.tensor_copy(flag, t_bank[0:1, 0:1]).then_inc(odd_link, 1)

            dve.wait_ge(const_ready, 3)
            nc.vector.tensor_copy(ones_r[:, :], ones[:, :]).then_inc(ones_ready, 1)
            prepare()
            step(0, first=True)
            with dve.Fori(1, LAST) as t:
                step(t)
            step(LAST, last=True)

            def update_first(t, c):
                old = stateT[:, 0, c * CW:(c + 1) * CW]
                n = 2 * (t * S_TWO + c * TWO)
                dve.wait_ge(gate_act, t * S_GATE + c * GATE + H * DB + 1)
                nc.vector.tensor_tensor(tmp[:, 0, :], gates[:, H, 0, :], old, ALU.subtract).then_inc(chain, 1)
                dve.wait_ge(chain, n + 1)
                nc.vector.tensor_tensor(tmp[:, 0, :], tmp[:, 0, :], gates[:, Z, 0, :], ALU.mult).then_inc(chain, 1)
                dve.wait_ge(chain, n + 2)
                nc.vector.tensor_tensor(old, old, tmp[:, 0, :], ALU.add).then_inc(state_new, 1)

            def mean_and_variance(c, between=None):
                dve.wait_ge(residual_ready, c + 1)
                for h in range(BC // 2):
                    n = c * BC + 2 * h
                    dve.wait_ge(o_done, n // 2 + 1)
                    nc.vector.tensor_tensor(y[:, n:n + 2, :], out_bank[c][h][:, :].rearrange("p (b d) -> p b d", d=D),
                                            x_res[:, n:n + 2, :], ALU.add).then_inc(o_read, 1)
                for n in range(c * BC, (c + 1) * BC):
                    if between is not None and n == c * BC + 2:
                        inverse(between)
                    dve.wait_ge(o_read, n // 2 + 1)
                    nc.vector.bn_stats(stats[:, n, :], y[:, n, :]).then_inc(stats_ready, 1)
                for n in range(c * BC, (c + 1) * BC):
                    dve.wait_ge(stats_ready, n + 1)
                    nc.vector.bn_aggr(mv[:, n, :], stats[:, n, :]).then_inc(aggr_ready, 1)

            def inverse(n):
                a, b = BATCHES[n]
                dve.wait_ge(std_ready, n + 1)
                nc.vector.reciprocal(rstd[:, a:b], std[:, a:b]).then_inc(rstd_ready, 1)
                dve.wait_ge(rstd_ready, n + 1)
                nc.vector.scalar_tensor_tensor(out=shift[:, a:b], in0=mv[:, a:b, 0], scalar=-1.0, in1=rstd[:, a:b],
                                               op0=ALU.mult, op1=ALU.mult).then_inc(shift_ready, 1)

            def normalize(m):
                nc.vector.tensor_scalar(y[:, m, :], y[:, m, :], mv[:, m, 0:1], rstd[:, m:m + 1],
                                        ALU.subtract, ALU.mult).then_inc(y_dve, 1)

            update_first(LAST, NC - 1)
            split_hidden(1)
            final_split(3)
            mean_and_variance(0)
            split_hidden(2)
            mean_and_variance(1)
            split_hidden(3)
            mean_and_variance(2, between=0)
            mean_and_variance(3, between=1)
            normalize(BY_DVE[0])
            inverse(2)
            normalize(BY_DVE[1])
            normalize(BY_DVE[2])


def general_path(nc, flag, x, adj, in_W, in_b, out_W, out_b, r_W, r_b, z_W, z_b, h_W, h_b,
                 o1_W, o1_b, o2_W, o2_b, out):
    N, D = x.shape
    NB = N // P
    NC = N // CW
    DB = D // P
    BC = CW // P
    NG = 3
    KB = NG * DB
    R, Z, H = range(NG)

    with ExitStack() as ctx:
        def sb(name, shape, dt=F32):
            return ctx.enter_context(nc.sbuf_tensor("g_" + name, shape, dt))

        def pb(name, shape, dt=F32):
            return ctx.enter_context(nc.psum_tensor("g_" + name, shape, dt))

        def sem(name):
            return ctx.enter_context(nc.semaphore("g_" + name))

        a_dram = nc.dram_tensor("a_dram", [N, N], F32, kind="Internal").ap()
        at_dram = nc.dram_tensor("at_dram", [N, N], F32, kind="Internal").ap()

        ident = sb("ident", [P, P])
        xb = sb("xb", [P, NB, D])
        stateT = sb("stateT", [P, DB, N])
        lin_raw = sb("lin_raw", [P, 4, DB, D])
        lin_T = sb("lin_T", [P, 4, DB, D])
        gate_raw = sb("gate_raw", [P, DB, NG * D])
        gate_T = sb("gate_T", [P, NG, KB, D])
        gate_b = sb("gate_b", [P, NG, DB])
        o1_bc = sb("o1_bc", [P, DB])
        io_b = sb("io_b", [P, 2 * D])
        o2_bb = sb("o2_bb", [P, D])
        s_io = sb("s_io", [P, NB, 2 * D])
        a_io = sb("a_io", [P, 4, CW])
        gates = sb("gates", [P, NG, DB, CW])
        rs = sb("rs", [P, DB, CW])
        tmp = sb("tmp", [P, DB, CW])
        tile = sb("tile", [P, 2, 2, 2, CW])
        y = sb("y", [P, BC, D])
        stats = sb("stats", [P, BC, 6])
        mv = sb("mv", [P, BC, 2])
        rstd = sb("rstd", [P, BC])
        araw = s_io[:, 0:4, :].bitcast(I32)
        af = s_io[:, 4:8, :]
        att = s_io[:, 8:12, :]

        bank = [pb(f"bank{i}", [P, CW]) for i in range(8)]

        loaded = sem("loaded")
        ident_zeroed = sem("ident_zeroed")
        ident_ready = sem("ident_ready")
        prep_done = sem("prep_done")
        prep_copied = sem("prep_copied")
        gate_loaded = sem("gate_loaded")
        gate_used = sem("gate_used")
        xb_ready = sem("xb_ready")
        araw_loaded = sem("araw_loaded")
        af_ready = sem("af_ready")
        at_done = sem("at_done")
        att_ready = sem("att_ready")
        a_stored = sem("a_stored")
        proj_done = sem("proj_done")
        proj_read = sem("proj_read")
        tile_loaded = [sem(f"tile_loaded{i}") for i in range(2)]
        tile_used = sem("tile_used")
        agg_done = sem("agg_done")
        agg_read = sem("agg_read")
        gate_done = sem("gate_done")
        gate_read = sem("gate_read")
        rs_ready = sem("rs_ready")
        link = sem("link")
        state_ready = sem("state_ready")
        hid_done = sem("hid_done")
        hid_ready = sem("hid_ready")
        o_done = sem("o_done")
        o_read = sem("o_read")
        var_ready = sem("var_ready")
        std_ready = sem("std_ready")
        y_ready = sem("y_ready")
        y_stored = sem("y_stored")

        block = ctx.enter_context(nc.Block())

        LOADS = 4 + 3 + 1 + 2 + 1 + 1
        x_v = x.rearrange("(b p) d -> p b d", p=P)

        @block.sync
        def _(sp):
            with sp.If(sp.value_load(flag, min_val=0, max_val=MISMATCHES) != 0):
                for n, w in enumerate((in_W, out_W, o1_W, o2_W)):
                    sp.dma_start(lin_raw[:, n], w.rearrange("(b p) k -> p b k", p=P)).then_inc(loaded, 16)
                for g, b in enumerate((r_b, z_b, h_b)):
                    sp.dma_start(gate_b[:, g], b.rearrange("(b p) -> p b", p=P), allow_slow_non_contiguous=True).then_inc(loaded, 16)
                sp.dma_start(o1_bc[:, :], o1_b.rearrange("(b p) -> p b", p=P), allow_slow_non_contiguous=True).then_inc(loaded, 16)
                sp.dma_start(io_b[:, 0:D], in_b.partition_broadcast(P)).then_inc(loaded, 16)
                sp.dma_start(io_b[:, D:], out_b.partition_broadcast(P)).then_inc(loaded, 16)
                sp.dma_start(o2_bb[:, :], o2_b.partition_broadcast(P)).then_inc(loaded, 16)
                sp.dma_start(xb[:, :, :], x_v).then_inc(loaded, 16)
                for g, w in enumerate((r_W, z_W, h_W)):
                    if g:
                        sp.wait_ge(gate_used, g)
                    sp.dma_start(gate_raw[:, :, :], w.rearrange("(b p) k -> p b k", p=P)).then_inc(gate_loaded, 16)
                with sp.Fori(0, NB) as b:
                    column = sp.snap(b * P)
                    sp.wait_ge(a_stored, 1 + b * 32)
                    sp.dma_start(araw, adj[bass.ds(b * P, P), :].rearrange("p (c w) -> p c w", c=NC)).then_inc(araw_loaded, 16)
                    sp.wait_ge(att_ready, 1 + (b + 1) * NC)
                    sp.dma_start(a_dram[bass.ds(b * P, P), :].rearrange("p (c w) -> p c w", c=NC), af).then_inc(a_stored, 16)
                    sp.dma_start(at_dram[:, bass.ds(column, P)].rearrange("(j p) i -> p j i", p=P),
                                 att.rearrange("p c (j i) -> p (c j) i", i=P)).then_inc(a_stored, 16)
                sp.wait_ge(a_stored, 1 + NB * 32)
                a_v = a_dram.rearrange("(j p) i -> p j i", p=P)
                at_v = at_dram.rearrange("(j p) i -> p j i", p=P)
                with sp.Fori(0, N_STEPS * NC) as q:
                    col = sp.snap((q % NC) * CW)
                    for j in range(NB // 2):
                        n = q * (NB // 2) + j
                        if j >= 2:
                            sp.wait_ge(tile_used, 1 + n - 1)
                        else:
                            sp.wait_ge(tile_used, 1 + q * (NB // 2))
                        for m, v in enumerate((at_v, a_v)):
                            sp.dma_start(tile[:, j % 2, m], v[:, 2 * j:2 * j + 2, bass.ds(col, CW)])\
                              .then_inc(tile_loaded[j % 2], 16)
                with sp.Fori(0, NC) as c:
                    sp.wait_ge(y_ready, (c + 1) * BC)
                    sp.dma_start(out.rearrange("(b p) d -> p b d", p=P)[:, bass.ds(c * BC, BC), :], y[:, :, :]).then_inc(y_stored, 16)
                sp.wait_ge(y_stored, 16 * NC)

        @block.gpsimd
        def _(pool):
            with pool.If(pool.value_load(flag, min_val=0, max_val=MISMATCHES) != 0):
                for s in (a_stored, tile_used, att_ready, state_ready, agg_read, gate_read, hid_ready, o_read, o_done):
                    pool.sem_inc(s, 1)
                nc.gpsimd.memset(ident[:, :], 0.0).then_inc(ident_zeroed, 1)
                pool.wait_ge(ident_zeroed, 1)
                nc.gpsimd.affine_select(out=ident[:, :], in_=ident[:, :], compare_op=ALU.not_equal, fill=1.0,
                                        base=0, pattern=[[-1, P]], channel_multiplier=1).then_inc(ident_ready, 1)

        @block.tensor
        def _(pe):
            with pe.If(pe.value_load(flag, min_val=0, max_val=MISMATCHES) != 0):
                pe.wait_ge(ident_ready, 1)
                pe.wait_ge(loaded, 16 * LOADS)
                n = 0
                for w in range(4):
                    for k in range(DB):
                        if n >= 8:
                            pe.wait_ge(prep_copied, n - 7)
                        for b in range(DB):
                            last = nc.tensor.transpose(bank[n % 8][:, b * P:(b + 1) * P], lin_raw[:, w, b, k * P:(k + 1) * P], ident[:, :])
                        last.then_inc(prep_done, 1)
                        n += 1
                for g in range(NG):
                    pe.wait_ge(gate_loaded, 16 * (g + 1))
                    for k in range(KB):
                        if n >= 8:
                            pe.wait_ge(prep_copied, n - 7)
                        for b in range(DB):
                            last = nc.tensor.transpose(bank[n % 8][:, b * P:(b + 1) * P], gate_raw[:, b, k * P:(k + 1) * P], ident[:, :])
                        last.then_inc(prep_done, 1)
                        n += 1
                for d in range(DB):
                    for c in range(NC):
                        pe.wait_ge(prep_copied, n - 7)
                        for b in range(BC):
                            last = nc.tensor.transpose(bank[n % 8][:, b * P:(b + 1) * P], xb[:, c * BC + b, d * P:(d + 1) * P], ident[:, :])
                        last.then_inc(prep_done, 1)
                        n += 1
                pe.wait_ge(prep_copied, n)
                with pe.Fori(0, NB) as b:
                    pe.wait_ge(af_ready, b + 1)
                    pe.wait_ge(att_ready, 1 + b * NC)
                    for c in range(NC):
                        for j in range(BC):
                            last = nc.tensor.transpose(bank[c][:, j * P:(j + 1) * P], af[:, c, j * P:(j + 1) * P], ident[:, :])
                        last.then_inc(at_done, 1)
                pe.wait_ge(att_ready, 1 + NB * NC)
                pe.wait_ge(a_stored, 1 + NB * 32)
                with pe.Fori(0, N_STEPS) as t:
                    pe.wait_ge(state_ready, 1 + t * NC * DB)
                    for b in range(NB):
                        if b >= 2:
                            pe.wait_ge(proj_read, t * NB + b - 1)
                        for k in range(DB):
                            last = nc.tensor.matmul(bank[b % 2][:, :], stateT[:, k, b * P:(b + 1) * P],
                                                    lin_T[:, 0:2, k, :], start=(k == 0), stop=(k == DB - 1))
                        last.then_inc(proj_done, 1)
                    with pe.Fori(0, NC) as c:
                        q = t * NC + c
                        pe.wait_ge(proj_read, (t + 1) * NB)
                        pe.wait_ge(agg_read, 1 + 4 * q)
                        for j in range(NB):
                            if j % 2 == 0:
                                pe.wait_ge(tile_loaded[j // 2 % 2], 32 * (q * (NB // 4) + j // 4 + 1))
                            for m in range(2):
                                for d in range(DB):
                                    last = nc.tensor.matmul(bank[2 + m * DB + d][:, :],
                                                            s_io[:, j, m * D + d * P:m * D + (d + 1) * P],
                                                            tile[:, j // 2 % 2, m, j % 2, :],
                                                            start=(j == 0), stop=(j == NB - 1))
                            if j == NB - 1:
                                last.then_inc(agg_done, 1)
                            if j % 2 == 1:
                                if j == NB - 1:
                                    pe.wait_ge(agg_done, q + 1)
                                    pe.sem_inc(tile_used, 1)
                                else:
                                    last.then_inc(tile_used, 1)
                        pe.wait_ge(agg_read, 1 + 4 * (q + 1))
                        for s in range(NG * DB):
                            g, e = s // DB, s % DB
                            pe.wait_ge(gate_read, 1 + q * NG * DB + (s - 1 if s >= 2 else 0))
                            for k in range(KB):
                                if k < 4:
                                    rhs = a_io[:, k, :]
                                elif g == H:
                                    if k == 4:
                                        pe.wait_ge(rs_ready, (q + 1) * DB)
                                    rhs = rs[:, k - 4, :]
                                else:
                                    rhs = stateT[:, k - 4, bass.ds(c * CW, CW)]
                                last = nc.tensor.matmul(bank[6 + s % 2][:, :], gate_T[:, g, k, e * P:(e + 1) * P], rhs,
                                                        start=(k == 0), stop=(k == KB - 1))
                            last.then_inc(gate_done, 1)
                pe.wait_ge(state_ready, 1 + N_STEPS * NC * DB)
                pe.wait_ge(gate_read, 1 + N_STEPS * NC * NG * DB)
                with pe.Fori(0, NC) as c:
                    pe.wait_ge(hid_ready, 1 + c * DB)
                    for e in range(DB):
                        for k in range(DB):
                            last = nc.tensor.matmul(bank[e][:, :], lin_T[:, 2, k, e * P:(e + 1) * P],
                                                    stateT[:, k, bass.ds(c * CW, CW)], start=(k == 0), stop=(k == DB - 1))
                        last.then_inc(hid_done, 1)
                    pe.wait_ge(hid_ready, 1 + (c + 1) * DB)
                    pe.wait_ge(o_read, 1 + c * BC)
                    for b in range(BC):
                        for k in range(DB):
                            last = nc.tensor.matmul(bank[2 + b][:, 0:D], rs[:, k, b * P:(b + 1) * P],
                                                    lin_T[:, 3, k, :], start=(k == 0), stop=(k == DB - 1))
                        last.then_inc(o_done, 1)

        @block.scalar
        def _(act):
            with act.If(act.value_load(flag, min_val=0, max_val=MISMATCHES) != 0):
                with act.Fori(0, N_STEPS * NC) as q:
                    act.wait_ge(state_ready, 1 + q * DB)
                    for s in range(NG * DB):
                        g, e = s // DB, s % DB
                        act.wait_ge(gate_done, q * NG * DB + s + 1)
                        nc.scalar.activation(gates[:, g, e, :], bank[6 + s % 2][:, :], ACT.Tanh if g == H else ACT.Sigmoid,
                                             bias=gate_b[:, g, e:e + 1]).then_inc(gate_read, 1)
                with act.Fori(0, NC) as c:
                    act.wait_ge(o_done, 1 + c * BC)
                    for e in range(DB):
                        act.wait_ge(hid_done, c * DB + e + 1)
                        nc.scalar.activation(rs[:, e, :], bank[e][:, :], ACT.Tanh, bias=o1_bc[:, e:e + 1]).then_inc(hid_ready, 1)
                    act.wait_ge(var_ready, c + 1)
                    nc.scalar.activation(rstd[:, :], mv[:, :, 1], ACT.Sqrt).then_inc(std_ready, 1)

        @block.vector
        def _(dve):
            with dve.If(dve.value_load(flag, min_val=0, max_val=MISMATCHES) != 0):
                n = 0
                for w in range(4):
                    for k in range(DB):
                        dve.wait_ge(prep_done, n + 1)
                        nc.vector.tensor_copy(lin_T[:, w, k, :], bank[n % 8][:, 0:D]).then_inc(prep_copied, 1)
                        n += 1
                for g in range(NG):
                    for k in range(KB):
                        dve.wait_ge(prep_done, n + 1)
                        if k == KB - 1:
                            dve.sem_inc(gate_used, 1)
                        nc.vector.tensor_copy(gate_T[:, g, k, :], bank[n % 8][:, 0:D]).then_inc(prep_copied, 1)
                        n += 1
                for d in range(DB):
                    for c in range(NC):
                        dve.wait_ge(prep_done, n + 1)
                        nc.vector.tensor_copy(stateT[:, d, c * CW:(c + 1) * CW], bank[n % 8][:, :]).then_inc(prep_copied, 1)
                        n += 1
                nc.vector.tensor_tensor(xb[:, :, :], xb[:, :, :], o2_bb[:, :].unsqueeze(1).broadcast_to([P, NB, D]), ALU.add).then_inc(xb_ready, 1)
                with dve.Fori(0, NB) as b:
                    dve.wait_ge(araw_loaded, 16 * (b + 1))
                    nc.vector.tensor_copy(af, araw).then_inc(af_ready, 1)
                    for c in range(NC):
                        dve.wait_ge(at_done, b * NC + c + 1)
                        nc.vector.tensor_copy(att[:, c, :], bank[c][:, :]).then_inc(att_ready, 1)
                dve.wait_ge(a_stored, 1 + NB * 32)
                with dve.Fori(0, N_STEPS) as t:
                    for b in range(NB):
                        dve.wait_ge(proj_done, t * NB + b + 1)
                        nc.vector.tensor_tensor(s_io[:, b, :], bank[b % 2][:, :], io_b[:, :], ALU.add).then_inc(proj_read, 1)
                    with dve.Fori(0, NC) as c:
                        q = t * NC + c
                        dve.wait_ge(agg_done, q + 1)
                        for k in range(4):
                            nc.vector.tensor_copy(a_io[:, k, :], bank[2 + k][:, :]).then_inc(agg_read, 1)
                        for e in range(DB):
                            dve.wait_ge(gate_read, 1 + q * NG * DB + e + 1)
                            nc.vector.tensor_tensor(rs[:, e, :], gates[:, R, e, :], stateT[:, e, bass.ds(c * CW, CW)], ALU.mult).then_inc(rs_ready, 1)
                        for e in range(DB):
                            se = stateT[:, e, bass.ds(c * CW, CW)]
                            u = 2 * (q * DB + e)
                            dve.wait_ge(gate_read, 1 + q * NG * DB + H * DB + e + 1)
                            nc.vector.tensor_tensor(tmp[:, e, :], gates[:, H, e, :], se, ALU.subtract).then_inc(link, 1)
                            dve.wait_ge(link, u + 1)
                            nc.vector.tensor_tensor(tmp[:, e, :], tmp[:, e, :], gates[:, Z, e, :], ALU.mult).then_inc(link, 1)
                            dve.wait_ge(link, u + 2)
                            nc.vector.tensor_tensor(se, se, tmp[:, e, :], ALU.add).then_inc(state_ready, 1)
                link0 = 2 * N_STEPS * NC * DB
                LN = 2 * BC + 1 + 2
                for c in range(NC):
                    if c:
                        dve.wait_ge(y_stored, 16 * c)
                    at = link0 + c * LN
                    for b in range(BC):
                        dve.wait_ge(o_done, 1 + c * BC + b + 1)
                        nc.vector.tensor_tensor(y[:, b, :], bank[2 + b][:, 0:D], xb[:, c * BC + b, :], ALU.add).then_inc(o_read, 1)
                    for b in range(BC):
                        dve.wait_ge(o_read, 1 + c * BC + b + 1)
                        nc.vector.bn_stats(stats[:, b, :], y[:, b, :]).then_inc(link, 1)
                    for b in range(BC):
                        dve.wait_ge(link, at + b + 1)
                        nc.vector.bn_aggr(mv[:, b, :], stats[:, b, :]).then_inc(link, 1)
                    dve.wait_ge(link, at + 2 * BC)
                    nc.vector.tensor_scalar(mv[:, :, 1], mv[:, :, 1], EPS, None, ALU.add).then_inc(var_ready, 1)
                    dve.wait_ge(std_ready, c + 1)
                    nc.vector.reciprocal(rstd[:, :], rstd[:, :]).then_inc(link, 3)
                    dve.wait_ge(link, at + 2 * BC + 3)
                    for b in range(BC):
                        nc.vector.tensor_scalar(y[:, b, :], y[:, b, :], mv[:, b, 0:1], rstd[:, b:b + 1], ALU.subtract, ALU.mult).then_inc(y_ready, 1)




def gnn_kernel(nc, *args):
    with nc.sbuf_tensor("flag", [1, 1], I32) as flag:
        fast_path(nc, flag[:, :], *args)
        general_path(nc, flag[:, :], *args)


_INS = ["x", "adj"] + ["L0_gnn_" + n for n in ("in_W", "in_b", "out_W", "out_b", "r_W", "r_b", "z_W", "z_b", "h_W", "h_b",
                                              "o1_W", "o1_b", "o2_W", "o2_b")]


def kernel(**inputs):
    import numpy as _np
    import concourse.bacc as _bacc
    from concourse import mybir as _mybir
    from concourse.bass_utils import run_bass_kernel_spmd as _run

    nc = _bacc.Bacc("TRN2", target_bir_lowering=False, num_devices=1)
    arrays, args = {}, []
    for name in _INS:
        a = _np.ascontiguousarray(inputs[name])
        arrays[f"in_{name}_dram"] = a
        args.append(nc.dram_tensor(f"in_{name}_dram", a.shape, _mybir.dt.from_np(a.dtype), kind="ExternalInput").ap())
    out = nc.dram_tensor("out_0_dram", inputs["x"].shape, _mybir.dt.float32, kind="ExternalOutput").ap()
    gnn_kernel(nc, *args, out)
    r = _run(nc, [arrays], core_ids=[0])
    return r.results[0]["out_0_dram"]
```
